# Optimizing a Trainium2 kernel written in Bass

```python
import numpy as np
import jax
import jax.numpy as jnp

def _softmax(x, axis=-1):
    return jax.nn.softmax(x, axis=axis)

def _gelu(x):
    return jax.nn.gelu(x, approximate=True)

def _silu(x):
    return jax.nn.silu(x)

def _sigmoid(x):
    return jax.nn.sigmoid(x)

def _layernorm(x, axis=-1, eps=1e-05):
    m = jnp.mean(x, axis=axis, keepdims=True)
    v = jnp.var(x, axis=axis, keepdims=True)
    return (x - m) / jnp.sqrt(v + eps)

def _scatter_add(tgt, idx, src, axis=0):
    return tgt.at[idx].add(src)

def _segment_sum(src, seg, n):
    return jax.ops.segment_sum(src, seg, n)
kernel_name = 'mk_pixart_resid_d1_seqx_r8_62c9c3'

def setup_inputs(seed: int=0):
    np.random.seed(seed)
    _w = jnp.asarray

    def _rec_inputs():
        import jax
        import jax.numpy as jnp
        _rk = jax.random.key(seed)
        x = 7.22e-05 + 1 * jax.random.normal(jax.random.fold_in(_rk, 1), (16, 128, 128), jnp.float32)
        _lenS = 128 - jax.random.randint(jax.random.fold_in(_rk, 7), (16,), 0, max(1, 128 // 4) + 1, jnp.int32)
        _lenS2 = 128 - jax.random.randint(jax.random.fold_in(_rk, 8), (16,), 0, max(1, 128 // 4) + 1, jnp.int32)
        _ctx_1024P = jax.random.normal(jax.random.fold_in(_rk, 11), (16, 16, 128), jnp.float32)
        _ctx_1024c = jax.random.dirichlet(jax.random.fold_in(_rk, 511), 0.3 * jnp.ones((16,), jnp.float32), (16, 128))
        _ctx_1024t = jnp.einsum('bsk,bkd->bsd', _ctx_1024c, _ctx_1024P)
        _ctx_1024t = _ctx_1024t * jax.lax.rsqrt(jnp.mean(jnp.square(_ctx_1024t)) + 1e-12) * 0.953939
        ctx_1024 = 5.54337e-07 + 0.0180436 * (_ctx_1024t + 0.3 * jax.random.normal(jax.random.fold_in(_rk, 611), (16, 128, 128), jnp.float32))
        cond_1024 = 0.000192168 + 0.0182672 * jax.random.normal(jax.random.fold_in(_rk, 12), (16, 128), jnp.float32)
        return (x, ctx_1024, cond_1024)
    x, ctx_1024, cond_1024 = _rec_inputs()

    def _L0_xcond_setup():
        import jax, jax.numpy as jnp
        import numpy as np
        B, S, H, L = (4, 256, 128, 4)
        CLAMP_LO, CLAMP_HI = (1e-08, 1.0 - 1e-08)
        LN_EPS = 1e-05

        def _linear_scan(a, b):

            def combine(left, right):
                al, bl = left
                ar, br = right
                return (ar * al, ar * bl + br)
            _, h = jax.lax.associative_scan(combine, (a, b), axis=1)
            return h

        def _mingru(x, Wz, bz, Wh, bh):
            z = jax.nn.sigmoid(jnp.einsum('bsi,hi->bsh', x, Wz) + bz)
            h_tilde = jnp.tanh(jnp.einsum('bsi,hi->bsh', x, Wh) + bh)
            a = jnp.clip(1.0 - z, CLAMP_LO, CLAMP_HI)
            return _linear_scan(a, z * h_tilde)

        def _layernorm(x, gamma, beta):
            mu = jnp.mean(x, axis=-1, keepdims=True)
            var = jnp.mean(jnp.square(x - mu), axis=-1, keepdims=True)
            return (x - mu) * jax.lax.rsqrt(var + LN_EPS) * gamma + beta

        def _stack(x, Wz, bz, Wh, bh, gamma, beta):
            h = x
            for i in range(L):
                h_new = _mingru(h, Wz[i], bz[i], Wh[i], bh[i])
                if i > 0:
                    h_new = h_new + h
                h = _layernorm(h_new, gamma, beta)
            return h
        key = jax.random.key(seed)
        ks = jax.random.split(key, 13)
        s = 1.0 / np.sqrt(H)
        u = lambda k, shape: jax.random.uniform(k, shape, jnp.float32, -s, s)
        return {'x': jax.random.normal(ks[0], (B, S, H), jnp.float32), 'fwd_Wz': u(ks[1], (L, H, H)), 'fwd_bz': u(ks[2], (L, H)), 'fwd_Wh': u(ks[3], (L, H, H)), 'fwd_bh': u(ks[4], (L, H)), 'bwd_Wz': u(ks[5], (L, H, H)), 'bwd_bz': u(ks[6], (L, H)), 'bwd_Wh': u(ks[7], (L, H, H)), 'bwd_bh': u(ks[8], (L, H)), 'fusion_W': u(ks[9], (H, 2 * H)), 'fusion_b': u(ks[10], (H,)), 'ln_gamma': jnp.ones((H,), jnp.float32), 'ln_beta': jnp.zeros((H,), jnp.float32)}
    _L0_xcond_all = _L0_xcond_setup()
    _L0_xcond_in = {k: v for k, v in _L0_xcond_all.items() if k in ('fusion_W', 'fusion_b', 'ln_gamma', 'ln_beta')}
    del _L0_xcond_all

    def _L0_ffn_setup():
        import jax, jax.numpy as jnp
        import numpy as np
        TOP_K = 2
        key = jax.random.key(seed)
        k0, k1, k2, k3 = jax.random.split(key, 4)
        B, T, C, E, F = (4, 256, 128, 8, 512)
        x = jax.random.normal(k0, (B, T, C), dtype=jnp.float32)
        gate_w = jax.random.normal(k1, (C, E), dtype=jnp.float32) * 0.02
        w1 = jax.random.normal(k2, (E, C, F), dtype=jnp.float32) * 0.02
        w2 = jax.random.normal(k3, (E, F, C), dtype=jnp.float32) * 0.02
        return {'x': x, 'gate_w': gate_w, 'w1': w1, 'w2': w2}
    _L0_ffn_all = _L0_ffn_setup()
    _L0_ffn_in = {k: v for k, v in _L0_ffn_all.items() if k in ('gate_w', 'w1', 'w2')}
    del _L0_ffn_all
    return {'x': x, 'ctx_1024': ctx_1024, 'cond_1024': cond_1024, 'L0_xcond_fusion_W': _L0_xcond_in['fusion_W'], 'L0_xcond_fusion_b': _L0_xcond_in['fusion_b'], 'L0_xcond_ln_gamma': _L0_xcond_in['ln_gamma'], 'L0_xcond_ln_beta': _L0_xcond_in['ln_beta'], 'L0_ffn_gate_w': _L0_ffn_in['gate_w'], 'L0_ffn_w1': _L0_ffn_in['w1'], 'L0_ffn_w2': _L0_ffn_in['w2']}

def reference(x, ctx_1024, cond_1024, L0_xcond_fusion_W, L0_xcond_fusion_b, L0_xcond_ln_gamma, L0_xcond_ln_beta, L0_ffn_gate_w, L0_ffn_w1, L0_ffn_w2):
    import jax
    import jax.numpy as jnp

    def _L0_xcond_ref(x, fwd_Wz, fwd_bz, fwd_Wh, fwd_bh, bwd_Wz, bwd_bz, bwd_Wh, bwd_bh, fusion_W, fusion_b, ln_gamma, ln_beta):
        import jax, jax.numpy as jnp
        import numpy as np
        B, S, H, L = (4, 256, 128, 4)
        CLAMP_LO, CLAMP_HI = (1e-08, 1.0 - 1e-08)
        LN_EPS = 1e-05

        def _linear_scan(a, b):

            def combine(left, right):
                al, bl = left
                ar, br = right
                return (ar * al, ar * bl + br)
            _, h = jax.lax.associative_scan(combine, (a, b), axis=1)
            return h

        def _mingru(x, Wz, bz, Wh, bh):
            z = jax.nn.sigmoid(jnp.einsum('bsi,hi->bsh', x, Wz) + bz)
            h_tilde = jnp.tanh(jnp.einsum('bsi,hi->bsh', x, Wh) + bh)
            a = jnp.clip(1.0 - z, CLAMP_LO, CLAMP_HI)
            return _linear_scan(a, z * h_tilde)

        def _layernorm(x, gamma, beta):
            mu = jnp.mean(x, axis=-1, keepdims=True)
            var = jnp.mean(jnp.square(x - mu), axis=-1, keepdims=True)
            return (x - mu) * jax.lax.rsqrt(var + LN_EPS) * gamma + beta

        def _stack(x, Wz, bz, Wh, bh, gamma, beta):
            h = x
            for i in range(L):
                h_new = _mingru(h, Wz[i], bz[i], Wh[i], bh[i])
                if i > 0:
                    h_new = h_new + h
                h = _layernorm(h_new, gamma, beta)
            return h
        h_fwd = _stack(x, fwd_Wz, fwd_bz, fwd_Wh, fwd_bh, ln_gamma, ln_beta)
        h_bwd = _stack(jnp.flip(x, axis=1), bwd_Wz, bwd_bz, bwd_Wh, bwd_bh, ln_gamma, ln_beta)
        h_bwd = jnp.flip(h_bwd, axis=1)
        h_comb = jnp.concatenate([h_fwd, h_bwd], axis=-1)
        return jnp.einsum('bsi,hi->bsh', h_comb, fusion_W) + fusion_b

    def _L0_ffn_ref(x, gate_w, w1, w2):
        import jax, jax.numpy as jnp
        import numpy as np
        TOP_K = 2
        E = gate_w.shape[-1]
        probs = jax.nn.softmax(x @ gate_w, axis=-1)
        topw, topi = jax.lax.top_k(probs, TOP_K)
        topw = topw / topw.sum(axis=-1, keepdims=True)
        combine = (jax.nn.one_hot(topi, E, dtype=x.dtype) * topw[..., None]).sum(axis=-2)

        def body(acc, params):
            w1_i, w2_i, cw = params
            h = jax.nn.gelu(x @ w1_i, approximate=False)
            return (acc + cw[..., None] * (h @ w2_i), None)
        acc0 = jnp.zeros_like(x)
        out, _ = jax.lax.scan(body, acc0, (w1, w2, jnp.moveaxis(combine, -1, 0)))
        return out
    x = x + _L0_xcond_ref(_layernorm(x, axis=-1), ctx_1024, cond_1024, ctx_1024, cond_1024, ctx_1024, cond_1024, ctx_1024, cond_1024, L0_xcond_fusion_W, L0_xcond_fusion_b, L0_xcond_ln_gamma, L0_xcond_ln_beta)
    x = x + _L0_ffn_ref(_layernorm(x, axis=-1), L0_ffn_gate_w, L0_ffn_w1, L0_ffn_w2)
    return x

_drawn_inputs = setup_inputs


def setup_inputs(seed=0):
    import zlib

    import numpy as np

    out = dict(_drawn_inputs(seed))
    spreads = {'L0_xcond_ln_gamma': (1.0, 0.2), 'L0_xcond_ln_beta': (0.0, 0.1)}
    factors = {}
    for name, (base, spread) in spreads.items():
        noise = np.random.default_rng([zlib.crc32(name.encode()), seed]).standard_normal(out[name].shape)
        drawn = base * np.exp(spread * noise) if base else spread * noise
        out[name] = jnp.asarray(drawn.astype(out[name].dtype))
    for name, factor in factors.items():
        out[name] = (out[name] * factor).astype(out[name].dtype)
    return out
```

```python
from contextlib import ExitStack

import concourse.bass as bass
from concourse import mybir

ALU = mybir.AluOpType
ACT = mybir.ActivationFunctionType
F32 = mybir.dt.float32
AX_X = mybir.AxisListType.X

P = 128
B = 16
H = 128
CH = 4
TPC = B // CH
N = TPC * P
L = 4
E = 8
F = 512
FC = F // P
UNITS = 2 * CH
NB = 4
LN_EPS = 1e-5
CLAMP_LO = 1e-8
CLAMP_HI = 1.0 - 1e-8


def program(nc, x, ctx_w, cond, fusion_w, fusion_b, ln_gamma, ln_beta, gate_w, w1, w2, out):
    with ExitStack() as stack:
        def sb(name, shape, dt=F32):
            return stack.enter_context(nc.sbuf_tensor(name, shape, dt))

        def sem(name):
            return stack.enter_context(nc.semaphore(name))

        banks = [stack.enter_context(nc.psum_tensor(f"bank{i}", [P, 512], F32)) for i in range(8)]
        pU, pC, pV, pR = banks[0:2], banks[2:4], banks[4:6], banks[6:8]

        xt = sb("x_tokens", [P, B, H])
        x0 = sb("x_normed", [P, B, H])
        x0T = sb("x_normed_T", [P, CH * N])
        ident = sb("ident", [P, P])
        cmat = sb("centering", [P, P])
        inv_h = sb("inv_h", [P, 1])
        ones_row = sb("ones_row", [1, P])
        w_raw = sb("w_raw", [P, L, H])
        wt_raw = sb("wt_raw", [P, L * H])
        wt_g = sb("wt_g", [P, L * H])
        wt_cur = sb("wt_cur", [P, H])
        gam = sb("gamma", [P, 1])
        bet = sb("beta", [P, 1])
        ngam = sb("neg_gamma", [P, 1])
        gam2 = sb("two_gamma", [P, 1])
        b_raw = sb("b_raw", [P, L])
        b_rows = sb("b_rows", [L, H])
        b_full = sb("b_full", [P, L])
        b_half = sb("b_neg_half", [P, L])
        cb = sb("centered_beta", [P, L])
        fw_raw = sb("fw_raw", [P, 2, H])
        fwt_raw = sb("fwt_raw", [P, 2, H])
        fwt_g = sb("fwt_g", [P, 2, H])
        fb_row = sb("fb_row", [1, H])
        fbias = sb("fbias", [P, H])
        gw = sb("gate_w", [P, E])
        w1s = sb("w1s", [P, E, F])
        w2s = sb("w2s", [P, E, FC, H])
        stats = sb("stats", [P, B, 6])
        mv = sb("mv", [P, B, 2])
        vpe = sb("vpe", [P, B])
        rs0 = sb("rs0", [P, B])
        mhalf = sb("minus_half", [P, B])

        T1 = sb("tanh_u", [P, NB, N])
        T2 = sb("tanh_mhalf_u", [P, NB, N])
        Ab = sb("decay", [P, NB, N])
        Bb = sb("drive", [P, NB, N])
        R = sb("resid", [P, NB, N])
        CS = sb("cent", [P, NB, N])
        SQ = sb("sq", [P, NB, N])
        ve = sb("var_eps", [P, NB, TPC])
        rs = sb("rstd", [P, NB, TPC])
        n = sb("n", [P, 2, CH * N])
        x2 = sb("x2", [P, B, H])
        g = sb("g", [P, 2, FC, N])
        lg = sb("logits", [P, B, E])
        pr = sb("probs", [P, B, E])
        t8 = sb("t8", [P, B, E])
        cand = sb("cand", [P, B, E])
        oh1 = sb("oh1", [P, B, E])
        oh2 = sb("oh2", [P, B, E])
        rank = sb("rank", [P, B, E])
        m1 = sb("m1", [P, B])
        m2 = sb("m2", [P, B])
        mx = sb("mx", [P, B])
        cw = sb("cw", [P, B, E])

        s_ldw, s_ldc, s_ldf, s_ldg, s_ld1 = (sem(s) for s in
            ("w_loaded", "cols_loaded", "fusion_loaded", "gate_loaded", "experts_loaded"))
        s_ldx = [sem(f"x_loaded{c}") for c in range(CH)]
        s_const = sem("constants_ready")
        s_dve = sem("vector_step")
        s_pool = sem("pool_step")
        s_xt = sem("x0T_ready")
        s_x0 = sem("x0_normed")
        s_tr = sem("transposed")
        s_wt = sem("weights_ready")
        s_wcur = sem("layer_weights_ready")
        s_prep = sem("prep_products")
        s_rs0 = sem("rstd0_ready")
        s_u, s_t, s_b, s_a, s_a0 = sem("u"), sem("t"), sem("b"), sem("a"), sem("a0")
        s_s, s_r, s_c, s_cs, s_sq = sem("s"), sem("r"), sem("c"), sem("cs"), sem("sq")
        s_v, s_ve, s_p, s_rb, s_n = sem("v"), sem("ve"), sem("p"), sem("rb"), sem("n_ready")
        s_f, s_x2 = sem("fused"), sem("x2_ready")
        s_up, s_g, s_dn, s_acc = sem("up"), sem("g_ready"), sem("down"), sem("acc")
        s_lg, s_route, s_e = sem("lg"), sem("route"), sem("expd")
        s_out = sem("stored")

        block = stack.enter_context(nc.Block())

        def unit(s, d):
            return s - d

        @block.sync
        def _(sp):
            xv = x.rearrange("b s d -> s b d")
            for c in range(CH):
                sp.dma_start(xt[:, c * TPC:(c + 1) * TPC, :], xv[:, c * TPC:(c + 1) * TPC, :]).then_inc(s_ldx[c], 16)
            sp.dma_start(w_raw[:], ctx_w[0:L].rearrange("l h i -> h l i")).then_inc(s_ldw, 16)
            for e in range(E):
                sp.dma_start(w1s[:, e, :], w1[e]).then_inc(s_ld1, 16)
                sp.dma_start(w2s[:, e], w2[e].rearrange("(f p) c -> p f c", p=P)).then_inc(s_ld1, 16)
            for c in range(CH):
                sp.wait_ge(s_acc, (c + 1) * E * TPC)
                sp.dma_start(out.rearrange("b s d -> s b d")[:, c * TPC:(c + 1) * TPC, :],
                             x2[:, c * TPC:(c + 1) * TPC, :]).then_inc(s_out, 16)
            sp.wait_ge(s_out, 16 * CH)

        def pidx(l, j):
            return j // 2 if l == 0 else CH + UNITS * (l - 1) + j

        @block.scalar
        def _(act):
            act.dma_start(gam[:], ln_gamma.rearrange("(p o) -> p o", o=1)).then_inc(s_ldc, 16)
            act.dma_start(bet[:], ln_beta.rearrange("(p o) -> p o", o=1)).then_inc(s_ldc, 16)
            act.dma_start(b_rows[:], cond[0:L]).then_inc(s_ldc, 16)
            act.dma_start(fw_raw[:], fusion_w.rearrange("o (d i) -> o d i", d=2)).then_inc(s_ldf, 16)
            act.dma_start(fb_row[:], fusion_b.rearrange("(o p) -> o p", o=1)).then_inc(s_ldf, 16)
            act.dma_start(gw[:], gate_w).then_inc(s_ldg, 16)
            for c in range(CH):
                act.wait_ge(s_tr, c + 1)
                nc.scalar.copy(x0T[:, c * N:(c + 1) * N], banks[2 * (c % 2)][:]).then_inc(s_xt, 1)
            act.wait_ge(s_wt, 5)

            def tanhs(l, j):
                p = pidx(l, j)
                act.wait_ge(s_u, p + 1)
                if not (isinstance(p, int) and p < NB):
                    act.wait_ge(s_b, p - NB + 1)
                    act.wait_ge(s_a, (UNITS * l + j - NB + 1) if l else 2 * (p - NB) + 2)
                q = p % NB
                nc.scalar.activation(T1[:, q], pU[p % 2][:], ACT.Tanh, bias=b_full[:, l:l + 1]).then_inc(s_t, 1)
                nc.scalar.activation(T2[:, q], pU[p % 2][:], ACT.Tanh, bias=b_half[:, l:l + 1], scale=-0.5).then_inc(s_t, 1)

            def centre(l, j):
                k = UNITS * l + j
                act.wait_ge(s_c, k + 1)
                if k >= NB:
                    act.wait_ge(s_n, k - NB + 1)
                    act.wait_ge(s_v, k - NB + 1)
                q = k % NB
                nc.scalar.activation(SQ[:, q], pC[k % 2][:], ACT.Square, bias=cb[:, l:l + 1]).then_inc(s_sq, 1)
                nc.scalar.activation(CS[:, q], pC[k % 2][:], ACT.Identity, bias=cb[:, l:l + 1]).then_inc(s_cs, 1)

            for s in range(UNITS * L + 4):
                if s < UNITS * L and (s >= UNITS or s % 2 == 0):
                    tanhs(s // UNITS, s % UNITS)
                k = s - 2
                if 0 <= k < UNITS * L:
                    centre(k // UNITS, k % UNITS)

            act.wait_ge(s_route, 2)
            nc.scalar.activation(pr[:], t8[:], ACT.Exp).then_inc(s_e, 1)
            for i in range(CH * E):
                for f in range(FC):
                    act.wait_ge(s_up, i * FC + f + 1)
                    if i >= 2 and f == 0:
                        act.wait_ge(s_dn, TPC * (i - 1))
                    nc.scalar.activation(g[:, i % 2, f], banks[f][:], ACT.Gelu).then_inc(s_g, 1)

        @block.gpsimd
        def _(pool):
            nc.gpsimd.memset(ident[:], 0.0).then_inc(s_pool, 1)
            nc.gpsimd.memset(mhalf[:], -0.5).then_inc(s_pool, 1)
            nc.gpsimd.memset(inv_h[:], 1.0 / H).then_inc(s_pool, 1)
            nc.gpsimd.memset(ones_row[:], 1.0).then_inc(s_pool, 1)
            nc.gpsimd.memset(cb[:], 0.0).then_inc(s_pool, 1)
            pool.wait_ge(s_pool, 5)
            nc.gpsimd.affine_select(out=ident[:], in_=ident[:], compare_op=ALU.not_equal, fill=1.0, base=0,
                                    pattern=[[-1, P]], channel_multiplier=1).then_inc(s_const, 1)
            nc.gpsimd.iota(rank[:], pattern=[[0, B], [-1, E]], base=E, channel_multiplier=0,
                           allow_small_or_imprecise_dtypes=True).then_inc(s_const, 1)
            for c in range(CH):
                pool.wait_ge(s_x0, c + 1)
                nc.gpsimd.tensor_tensor(rs0[:, c * TPC:(c + 1) * TPC], vpe[:, c * TPC:(c + 1) * TPC],
                                        mhalf[:, 0:TPC], ALU.pow).then_inc(s_rs0, 1)
            pool.wait_ge(s_wt, 4)
            nc.gpsimd.tensor_copy(wt_cur[:], wt_raw[:, 0:H]).then_inc(s_wcur, 1)

            def decay(l, j):
                k = UNITS * l + j
                p = pidx(l, j)
                pool.wait_ge(s_t, 2 * p + 2)
                if k >= NB:
                    pool.wait_ge(s_r, k - NB + 1)
                q, d = k % NB, j % 2
                nc.gpsimd.tensor_scalar(Ab[:, q], T2[:, p % NB], 0.5, 0.5, ALU.mult, ALU.add).then_inc(s_a0, 1)
                pool.wait_ge(s_a0, 2 * k + 1)
                nc.gpsimd.tensor_scalar(Ab[:, q], Ab[:, q], CLAMP_HI, CLAMP_LO, ALU.min, ALU.max).then_inc(s_a0, 1)
                pool.wait_ge(s_a0, 2 * k + 2)
                first = 0 if d == 0 else P - 1
                nc.gpsimd.memset(Ab[:, q, first::P], 0.0).then_inc(s_a, 1)

            def power(l, j):
                k = UNITS * l + j
                pool.wait_ge(s_ve, k + 1)
                if k >= NB:
                    pool.wait_ge(s_rb, k - NB + 1)
                q = k % NB
                nc.gpsimd.tensor_tensor(rs[:, q], ve[:, q], mhalf[:, 0:TPC], ALU.pow).then_inc(s_p, 1)

            for s in range(UNITS * L + 4):
                l, j = s // UNITS, s % UNITS
                if 0 < l < L and j == 0:
                    pool.wait_ge(s_u, pidx(l - 1, UNITS - 1) + 1)
                    nc.gpsimd.tensor_copy(wt_cur[:], wt_g[:, l * H:(l + 1) * H]).then_inc(s_wcur, 1)
                if l < L:
                    decay(l, j)
                k = s - 3
                if 0 <= k < UNITS * L:
                    power(k // UNITS, k % UNITS)
            for c in range(CH):
                pool.wait_ge(s_x2, B + c + 1)
                nc.gpsimd.tensor_tensor(rs0[:, c * TPC:(c + 1) * TPC], vpe[:, c * TPC:(c + 1) * TPC],
                                        mhalf[:, 0:TPC], ALU.pow).then_inc(s_rs0, 1)

        @block.vector
        def _(dve):
            steps = [0]

            def done(ins):
                steps[0] += 1
                ins.then_inc(s_dve, 1)

            def settle():
                dve.wait_ge(s_dve, steps[0])

            def link(ins):
                done(ins)
                settle()

            def layernorm(src, c):
                for t in range(c * TPC, (c + 1) * TPC):
                    done(nc.vector.bn_stats(stats[:, t], src[:, t]))
                settle()
                for t in range(c * TPC, (c + 1) * TPC):
                    done(nc.vector.bn_aggr(mv[:, t], stats[:, t]))
                settle()
                return nc.vector.tensor_scalar(vpe[:, c * TPC:(c + 1) * TPC], mv[:, c * TPC:(c + 1) * TPC, 1], LN_EPS,
                                               None, ALU.add)

            for c in range(CH):
                dve.wait_ge(s_ldx[c], 16)
                layernorm(xt, c).then_inc(s_x0, 1)
            for c in range(CH):
                dve.wait_ge(s_rs0, c + 1)
                for t in range(c * TPC, (c + 1) * TPC):
                    ins = nc.vector.tensor_scalar(x0[:, t], xt[:, t], mv[:, t, 0:1], rs0[:, t:t + 1], ALU.subtract, ALU.mult)
                ins.then_inc(s_x0, 1)
            dve.wait_ge(s_ldc, 48)
            dve.wait_ge(s_const, 2)
            done(nc.vector.tensor_scalar(ngam[:], gam[:], -1.0, None, ALU.mult))
            done(nc.vector.tensor_scalar(gam2[:], gam[:], 2.0, None, ALU.mult))
            link(nc.vector.tensor_scalar(cmat[:], ident[:], -1.0 / H, None, ALU.add))
            nc.vector.tensor_copy(x2[:, 0, 2:3], ident[:, 0:1]).then_inc(s_wt, 1)
            dve.wait_ge(s_prep, 1)
            done(nc.vector.tensor_copy(wt_raw[:], banks[4][:]))
            link(nc.vector.tensor_scalar(wt_g[:], banks[4][:], ngam[:], None, ALU.mult))
            nc.vector.tensor_copy(x2[:, 0, 0:1], ident[:, 0:1]).then_inc(s_wt, 1)
            dve.wait_ge(s_prep, 2)
            done(nc.vector.tensor_copy(fwt_raw[:], banks[5][:, 0:2 * H].rearrange("p (d o) -> p d o", d=2)))
            link(nc.vector.tensor_scalar(fwt_g[:], banks[5][:, 0:2 * H].rearrange("p (d o) -> p d o", d=2), ngam[:], None, ALU.mult))
            nc.vector.tensor_copy(x2[:, 0, 1:2], ident[:, 0:1]).then_inc(s_wt, 1)
            dve.wait_ge(s_prep, 3)
            link(nc.vector.tensor_copy(b_raw[:], banks[6][:, 8:8 + L]))
            link(nc.vector.tensor_copy(b_full[:, 0:1], b_raw[:, 0:1]))
            link(nc.vector.tensor_tensor(b_full[:, 1:L], banks[6][:, 1:L], b_raw[:, 1:L], ALU.add))
            link(nc.vector.tensor_scalar(cb[:, 1:L], banks[6][:, L:L + 1].to_broadcast([P, L - 1]), -2.0, None, ALU.mult))
            nc.vector.tensor_scalar(b_half[:], b_full[:], -0.5, None, ALU.mult).then_inc(s_wt, 1)
            dve.wait_ge(s_prep, 4)
            nc.vector.tensor_copy(fbias[:], banks[7][:, 0:H]).then_inc(s_wt, 1)
            dve.wait_ge(s_wt, 5)

            def drive(l, j):
                p = pidx(l, j)
                dve.wait_ge(s_t, 2 * p + 2)
                q = p % NB
                nc.vector.scalar_tensor_tensor(out=Bb[:, q], in0=T2[:, q], scalar=-1.0, in1=T1[:, q],
                                               op0=ALU.add, op1=ALU.mult).then_inc(s_b, 1)

            def scan(l, j):
                k, p = UNITS * l + j, pidx(l, j)
                dve.wait_ge(s_b, p + 1)
                dve.wait_ge(s_a, k + 1)
                if k >= NB:
                    dve.wait_ge(s_c, k - NB + 1)
                q, d, c = k % NB, j % 2, j // 2
                way = slice(None) if d == 0 else slice(None, None, -1)
                a_, b_, o_ = (v[:, way] for v in (Ab[:, q], Bb[:, p % NB], R[:, q]))
                ins = nc.vector.tensor_tensor_scan(out=o_, data0=a_, data1=b_, initial=0.0, op0=ALU.mult, op1=ALU.add)
                if k < UNITS - 1:
                    ins.then_inc(s_r, 1)
                    return
                ins.then_inc(s_s, 1)
                dve.wait_ge(s_s, k - UNITS + 2)
                if l == 0:
                    nc.vector.tensor_copy(R[:, q], R[:, q]).then_inc(s_r, 1)
                else:
                    nc.vector.scalar_tensor_tensor(out=R[:, q], in0=n[:, d, c * N:(c + 1) * N], scalar=gam2[:],
                                               in1=R[:, q], op0=ALU.mult, op1=ALU.add).then_inc(s_r, 1)

            def addeps(l, j):
                k = UNITS * l + j
                dve.wait_ge(s_v, k + 1)
                if k >= NB:
                    dve.wait_ge(s_p, k - NB + 1)
                nc.vector.tensor_scalar(ve[:, k % NB], pV[k % 2][:, 0:TPC], 4 * LN_EPS, None, ALU.add).then_inc(s_ve, 1)

            def norm(l, j):
                k = UNITS * l + j
                q, d, c = k % NB, j % 2, j // 2
                dve.wait_ge(s_rb, k + 1)
                dve.wait_ge(s_cs, k + 1)
                nc.vector.tensor_tensor(n[:, d, c * N:(c + 1) * N], CS[:, q], pR[k % 2][:], ALU.mult).then_inc(s_n, 1)

            K = UNITS * L
            for s in range(K + 4):
                if 0 <= s - 1 < K:
                    scan((s - 1) // UNITS, (s - 1) % UNITS)
                if s < K and (s >= UNITS or s % 2 == 0):
                    drive(s // UNITS, s % UNITS)
                if 0 <= s - 3 < K:
                    addeps((s - 3) // UNITS, (s - 3) % UNITS)
                if 0 <= s - 4 < K:
                    norm((s - 4) // UNITS, (s - 4) % UNITS)

            for t in range(B):
                link(nc.vector.tensor_tensor(x2[:, t], xt[:, t], fbias[:], ALU.add))
                dve.wait_ge(s_f, t + 1)
                nc.vector.tensor_tensor(x2[:, t], x2[:, t], banks[t % 2][:, 0:H], ALU.add).then_inc(s_x2, 1)
            dve.wait_ge(s_x2, B)
            for c in range(CH):
                layernorm(x2, c).then_inc(s_x2, 1)
            for c in range(CH):
                dve.wait_ge(s_rs0, CH + c + 1)
                for t in range(c * TPC, (c + 1) * TPC):
                    ins = nc.vector.tensor_scalar(x0[:, t], x2[:, t], mv[:, t, 0:1], rs0[:, t:t + 1], ALU.subtract, ALU.mult)
                ins.then_inc(s_x0, 1)
            for c in range(CH):
                dve.wait_ge(s_tr, CH + c + 1)
                nc.vector.tensor_copy(x0T[:, c * N:(c + 1) * N], banks[2 + c % 2][:]).then_inc(s_xt, 1)
            dve.wait_ge(s_lg, 1)
            link(nc.vector.tensor_copy(lg[:], banks[4][:, 0:B * E].rearrange("p (b e) -> p b e", e=E)))

            def col(v):
                return v[:].unsqueeze(2).to_broadcast([P, B, E])

            link(nc.vector.tensor_reduce(mx[:], lg[:], AX_X, ALU.max))
            nc.vector.tensor_tensor(t8[:], lg[:], col(mx), ALU.subtract).then_inc(s_route, 2)
            dve.wait_ge(s_e, 1)
            link(nc.vector.tensor_reduce(mx[:], pr[:], AX_X, ALU.add))
            link(nc.vector.reciprocal(mx[:], mx[:]))
            link(nc.vector.tensor_tensor(pr[:], pr[:], col(mx), ALU.mult))

            def pick(m, oh):
                link(nc.vector.tensor_reduce(m[:], pr[:], AX_X, ALU.max))
                link(nc.vector.tensor_tensor(t8[:], pr[:], col(m), ALU.is_equal))
                link(nc.vector.tensor_tensor(cand[:], t8[:], rank[:], ALU.mult))
                link(nc.vector.tensor_reduce(mx[:], cand[:], AX_X, ALU.max))
                link(nc.vector.tensor_tensor(oh[:], cand[:], col(mx), ALU.is_equal))

            pick(m1, oh1)
            link(nc.vector.scalar_tensor_tensor(out=pr[:], in0=oh1[:], scalar=-2.0, in1=pr[:], op0=ALU.mult, op1=ALU.add))
            pick(m2, oh2)
            link(nc.vector.tensor_tensor(mx[:], m1[:], m2[:], ALU.add))
            link(nc.vector.reciprocal(mx[:], mx[:]))
            done(nc.vector.tensor_tensor(m1[:], m1[:], mx[:], ALU.mult))
            link(nc.vector.tensor_tensor(m2[:], m2[:], mx[:], ALU.mult))
            done(nc.vector.tensor_tensor(oh1[:], oh1[:], col(m1), ALU.mult))
            link(nc.vector.tensor_tensor(oh2[:], oh2[:], col(m2), ALU.mult))
            link(nc.vector.tensor_tensor(cw[:], oh1[:], oh2[:], ALU.add))
            for i in range(CH * E):
                c, e = i // E, i % E
                for t in range(TPC):
                    m = i * TPC + t
                    dve.wait_ge(s_dn, m + 1)
                    if m >= TPC:
                        dve.wait_ge(s_acc, m - TPC + 1)
                    o = x2[:, c * TPC + t]
                    nc.vector.scalar_tensor_tensor(out=o, in0=banks[4 + m % 4][:, 0:H], scalar=cw[:, c * TPC + t, e:e + 1],
                                                   in1=o, op0=ALU.mult, op1=ALU.add).then_inc(s_acc, 1)

        @block.tensor
        def _(pe):
            mm, tr = nc.tensor.matmul, nc.tensor.transpose
            pe.wait_ge(s_const, 1)
            pe.wait_ge(s_ldw, 16)
            for l in range(L):
                ins = tr(banks[4][:, l * H:(l + 1) * H], w_raw[:, l, :], ident[:])
            ins.then_inc(s_prep, 1)
            pe.wait_ge(s_ldf, 32)
            for d in range(2):
                ins = tr(banks[5][:, d * H:(d + 1) * H], fw_raw[:, d, :], ident[:])
            ins.then_inc(s_prep, 1)
            for c in range(CH):
                pe.wait_ge(s_x0, CH + c + 1)
                if c >= 2:
                    pe.wait_ge(s_xt, c - 1)
                for t in range(TPC):
                    ins = tr(banks[2 * (c % 2)][:, t * P:(t + 1) * P], x0[:, c * TPC + t, :], ident[:])
                ins.then_inc(s_tr, 1)
            pe.wait_ge(s_ldc, 48)
            pe.wait_ge(s_wt, 2)
            mm(banks[6][:, 8:8 + L], b_rows[:], ident[0:L, 0:L], start=True, stop=True)
            for l in range(1, L):
                mm(banks[6][:, l:l + 1], wt_raw[:, l * H:(l + 1) * H], bet[:], start=True, stop=True)
            mm(banks[6][:, L:L + 1], cmat[:], bet[:], start=True, stop=True).then_inc(s_prep, 1)
            pe.wait_ge(s_wt, 3)
            for d in range(2):
                mm(banks[7][:, 0:H], bet[:].to_broadcast([P, P]), fwt_raw[:, d, :], start=(d == 0), stop=False)
            mm(banks[7][:, 0:H], ones_row[:], fb_row[:], start=False, stop=True).then_inc(s_prep, 1)
            pe.wait_ge(s_wt, 5)

            def project(l, j):
                p = pidx(l, j)
                d, c = j % 2, j // 2
                if l == 0:
                    pe.wait_ge(s_xt, CH)
                    if c >= 2:
                        pe.wait_ge(s_t, 2 * (p - 1))
                    src = x0T[:, c * N:(c + 1) * N]
                else:
                    pe.wait_ge(s_n, UNITS * (l - 1) + j + 1)
                    pe.wait_ge(s_t, 2 * (p - 1))
                    src = n[:, d, c * N:(c + 1) * N]
                pe.wait_ge(s_wcur, l + 1)
                mm(pU[p % 2][:], wt_cur[:], src, start=True, stop=True).then_inc(s_u, 1)

            def centre(l, j):
                k = UNITS * l + j
                pe.wait_ge(s_r, k + 1)
                if k >= 2:
                    pe.wait_ge(s_cs, k - 1)
                mm(pC[k % 2][:], cmat[:], R[:, k % NB], start=True, stop=True).then_inc(s_c, 1)

            def variance(l, j):
                k = UNITS * l + j
                pe.wait_ge(s_sq, k + 1)
                if k >= 2:
                    pe.wait_ge(s_ve, k - 1)
                for t in range(TPC):
                    ins = mm(pV[k % 2][:, t:t + 1], SQ[:, k % NB, t * P:(t + 1) * P], inv_h[:], start=True, stop=True)
                ins.then_inc(s_v, 1)

            def spread(l, j):
                k = UNITS * l + j
                pe.wait_ge(s_p, k + 1)
                if k >= 2:
                    pe.wait_ge(s_n, k - 1)
                for t in range(TPC):
                    ins = mm(pR[k % 2][:, t * P:(t + 1) * P], rs[:, k % NB, t:t + 1].to_broadcast([P, P]), ident[:],
                             start=True, stop=True)
                ins.then_inc(s_rb, 1)

            K = UNITS * L
            for s in range(K + 4):
                if s < K and (s >= UNITS or s % 2 == 0):
                    project(s // UNITS, s % UNITS)
                if 0 <= s - 2 < K:
                    centre((s - 2) // UNITS, (s - 2) % UNITS)
                if 0 <= s - 3 < K:
                    variance((s - 3) // UNITS, (s - 3) % UNITS)
                if 0 <= s - 4 < K:
                    spread((s - 4) // UNITS, (s - 4) % UNITS)
            pe.wait_ge(s_n, K)
            for t in range(B):
                if t >= 2:
                    pe.wait_ge(s_x2, t - 1)
                for d in range(2):
                    ins = mm(banks[t % 2][:, 0:H], n[:, d, t * P:(t + 1) * P], fwt_g[:, d, :], start=(d == 0), stop=(d == 1))
                ins.then_inc(s_f, 1)
            for c in range(CH):
                pe.wait_ge(s_x0, 3 * CH + c + 1 - CH)
                if c >= 2:
                    pe.wait_ge(s_xt, CH + c - 1)
                for t in range(TPC):
                    ins = tr(banks[2 + c % 2][:, t * P:(t + 1) * P], x0[:, c * TPC + t, :], ident[:])
                ins.then_inc(s_tr, 1)
            pe.wait_ge(s_ldg, 16)
            pe.wait_ge(s_xt, 2 * CH)
            for t in range(B):
                ins = mm(banks[4][:, t * E:(t + 1) * E], x0T[:, t * P:(t + 1) * P], gw[:], start=True, stop=True)
            ins.then_inc(s_lg, 1)
            pe.wait_ge(s_ld1, 32 * E)
            pe.wait_ge(s_route, 2)

            def up(i):
                c, e = i // E, i % E
                for f in range(FC):
                    if i >= 1:
                        pe.wait_ge(s_g, (i - 1) * FC + f + 1)
                    mm(banks[f][:], w1s[:, e, f * P:(f + 1) * P], x0T[:, c * N:(c + 1) * N], start=True, stop=True).then_inc(s_up, 1)

            def down(i):
                c, e = i // E, i % E
                pe.wait_ge(s_g, FC * (i + 1))
                for t in range(TPC):
                    m = i * TPC + t
                    if m >= 4:
                        pe.wait_ge(s_acc, m - 3)
                    for f in range(FC):
                        ins = mm(banks[4 + m % 4][:, 0:H], g[:, i % 2, f, t * P:(t + 1) * P], w2s[:, e, f, :],
                                 start=(f == 0), stop=(f == FC - 1))
                    ins.then_inc(s_dn, 1)

            up(0)
            for i in range(CH * E):
                if i + 1 < CH * E:
                    up(i + 1)
                down(i)


_INS = ["x", "ctx_1024", "cond_1024", "L0_xcond_fusion_W", "L0_xcond_fusion_b", "L0_xcond_ln_gamma", "L0_xcond_ln_beta",
        "L0_ffn_gate_w", "L0_ffn_w1", "L0_ffn_w2"]


def kernel(**inputs):
    import numpy as np
    import concourse.bacc as bacc
    from concourse.bass_utils import run_bass_kernel_spmd

    nc = bacc.Bacc("TRN2", target_bir_lowering=False, num_devices=1)
    arrays, args = {}, []
    for name in _INS:
        a = np.ascontiguousarray(inputs[name])
        arrays[f"in_{name}"] = a
        args.append(nc.dram_tensor(f"in_{name}", a.shape, mybir.dt.from_np(a.dtype), kind="ExternalInput").ap())
    args.append(nc.dram_tensor("out", (B, P, H), F32, kind="ExternalOutput").ap())
    program(nc, *args)
    return run_bass_kernel_spmd(nc, [arrays], core_ids=[0]).results[0]["out"]
```

```python
from contextlib import ExitStack

import concourse.bass as bass
from concourse import mybir

ALU = mybir.AluOpType
ACT = mybir.ActivationFunctionType
F32 = mybir.dt.float32
F32R = mybir.dt.float32r
BF16 = mybir.dt.bfloat16
U32 = mybir.dt.uint32
AX_X = mybir.AxisListType.X

P = 128
B = 16
H = 128
CH = 4
TPC = B // CH
N = TPC * P
L = 4
E = 8
F = 512
FC = F // P
UNITS = 2 * CH
NB = 3
BLK = 40
DUMMY = BLK - 2 * B
REG = B * P + P
RW = H + 2
DEST, WGT = H, H + 1
Q = 8
LN_EPS = 1e-5
CLAMP_LO = 1e-8
CLAMP_HI = 1.0 - 1e-8


def after(engine, semaphore, count):
    if not (isinstance(count, int) and count <= 0):
        engine.wait_ge(semaphore, count)


def program(nc, x, ctx_w, cond, fusion_w, fusion_b, ln_gamma, ln_beta, gate_w, w1, w2, out, rows, yrows):
    with ExitStack() as stack:
        def sb(name, shape, dt=F32):
            return stack.enter_context(nc.sbuf_tensor(name, shape, dt))

        def sem(name):
            return stack.enter_context(nc.semaphore(name))

        banks = [stack.enter_context(nc.psum_tensor(f"bank{i}", [P, 512], F32)) for i in range(8)]
        pU, pC, pR = banks[0:2], banks[2:4], banks[6:8]
        pV, pX = banks[4], banks[5]
        post_bank = [pX, pU[0], pX, pU[1]]

        xt = sb("x_tokens", [P, B, H])
        x2 = sb("x2", [P, B, H])
        x0 = x2
        x0T = sb("x_normed_T", [P, CH * N])
        ident = sb("ident", [P, P])
        cmat = sb("centering", [P, P])
        before = sb("tokens_before", [P, P], BF16)
        ones_bf = sb("ones_bf", [P, P], BF16)
        inv_h = sb("inv_h", [P, 1])
        ones_row = sb("ones_row", [1, P])
        w_raw = sb("w_raw", [P, L, H])
        wt_raw = sb("wt_raw", [P, L * H])
        wt_g = sb("wt_g", [P, L * H])
        gam = sb("gamma", [P, 1])
        bet = sb("beta", [P, 1])
        ngam = sb("neg_gamma", [P, 1])
        gam2 = sb("two_gamma", [P, 1])
        b_rows = sb("b_rows", [L, H])
        b_raw = sb("b_raw", [P, L])
        b_full = sb("b_full", [P, L])
        b_half = sb("b_neg_half", [P, L])
        cb = sb("centered_beta", [P, L])
        fw_raw = sb("fw_raw", [P, 2, H])
        fwt_raw = sb("fwt_raw", [P, 2, H])
        fwt_g = sb("fwt_g", [P, 2, H])
        fb_row = sb("fb_row", [1, H])
        fbias = sb("fbias", [P, H])
        gw = sb("gate_w", [P, E])
        wst = sb("w_stage", [P, 2, F])
        w1s = sb("w1_split", [P, E, 2, F], F32R)
        w2s = sb("w2_split", [P, E, FC, 2, P], F32R)
        stats = sb("stats", [P, B, 6])
        mv = sb("mv", [P, B, 2])
        vpe = sb("vpe", [P, B])
        rs0 = sb("rs0", [P, B])
        mhalf = sb("minus_half", [P, TPC])

        T1 = sb("tanh_u", [P, NB, N])
        T2 = sb("tanh_mhalf_u", [P, NB, N])
        Ab = sb("decay", [P, NB, N])
        Bb = sb("drive", [P, NB, N])
        R = sb("resid", [P, NB, N])
        CS = sb("cent", [P, NB, N])
        SQ = sb("sq", [P, NB, N])
        ve = sb("var_eps", [P, NB, TPC])
        rs = sb("rstd", [P, NB, TPC])
        n = sb("n", [P, 2, CH * N])
        yall = n[:].rearrange("p d (c t) -> p (d c t)", c=CH).rearrange("p (c t k h) -> p c t k h", c=CH, t=TPC, k=2)

        xr = sb("routed_rows", [P, 2, B, RW])
        pad = sb("pad_rows", [P, E + DUMMY, RW])
        pr = sb("probs", [P, TPC, E])
        t8 = sb("t8", [P, TPC, E])
        cand = sb("cand", [P, TPC, E])
        oh = [sb(f"one_hot{k}", [P, TPC, E]) for k in range(2)]
        rank = sb("rank", [P, TPC, E])
        eoff = sb("expert_start", [P, TPC, E])
        mk = [sb(f"top{k}", [P, TPC]) for k in range(2)]
        mx = sb("mx", [P, TPC])
        M = sb("chosen", [P, B, E], BF16)
        Mc = sb("chosen_before", [P, B + 1, E], BF16)
        slotf = sb("slot_f", [P, 2, TPC])
        slot = sb("slot", [P, CH, 2, TPC], U32)
        cnt = sb("cnt", [1, E])
        c128 = sb("c128", [1, E, B])
        gtc = sb("gtc", [1, E, B])
        nblk = sb("nblk", [1, E])
        ones8 = sb("ones8", [1, E])
        endb = sb("endb", [1, E])
        dlt = sb("dlt", [1, E])
        jj = sb("jj", [1, BLK, E])
        ge = sb("ge", [1, BLK, E])
        tj = sb("tj", [1, BLK])
        tr_ = sb("tr_", [1, BLK])
        eid = sb("block_expert", [1, BLK], U32)
        brow = sb("block_row", [1, BLK], U32)
        prow = sb("pad_row", [1, E], U32)

        xb = Ab[:].rearrange("p k n -> p (k n)")[:, 0:Q * RW].rearrange("p (q r) -> p q r", q=Q)
        xh, xl = sb("xh", [P, 2, P], F32R), sb("xl", [P, 2, P], F32R)
        g = T1
        gh, gl = sb("gh", [P, 2, F], F32R), sb("gl", [P, 2, F], F32R)
        yl = sb("y_low", [P, 2, H])
        meta = sb("meta", [P, Q, 2])
        yb = T2[:, 0:2, :].rearrange("p t (q h) -> p (t q) h", q=Q // 2)

        s_ldw, s_ldc, s_ldf, s_ldg = (sem(s) for s in ("w_loaded", "cols_loaded", "fusion_loaded", "gate_loaded"))
        s_ldx = [sem(f"x_loaded{c}") for c in range(CH)]
        s_lde = [sem(f"experts_loaded{c}") for c in range(2)]
        s_high, s_split, s_padw = sem("weights_high"), sem("weights_split"), sem("pads_written")
        s_const, s_dve, s_pool = sem("constants_ready"), sem("vector_step"), sem("pool_step")
        s_st, s_x0, s_xt, s_tr = sem("stats0"), sem("x0_normed"), sem("x0T_ready"), sem("transposed")
        s_prep, s_wt, s_rs0 = sem("prep_products"), sem("prep_copied"), sem("rstd0_ready")
        s_u, s_t, s_b, s_a, s_a0 = sem("u"), sem("t"), sem("b"), sem("a"), sem("a0")
        s_s, s_r, s_c, s_cs, s_sq = sem("s"), sem("r"), sem("c"), sem("cs"), sem("sq")
        s_v, s_ve, s_p, s_rb, s_n = sem("v"), sem("ve"), sem("p"), sem("rb"), sem("n_ready")
        s_f, s_x2, s_st2, s_xn, s_tr2, s_xt2, s_xr = (sem(v) for v in
            ("fused", "x2_ready", "stats2", "xn", "tr2", "xt2", "xr"))
        s_lg, s_sub, s_exp, s_m, s_pos, s_slot = (sem(v) for v in ("lg", "sub", "exp", "m", "pos", "slots"))
        s_pads, s_scat, s_cnt, s_tab = sem("pads_stored"), sem("scattered"), sem("counted"), sem("table_ready")
        s_xb = [sem(f"xb{q}") for q in range(Q)]
        s_sc = [sem(f"y_scattered{q}") for q in range(Q)]
        s_xtr, s_xh, s_xl, s_up, s_g, s_gtr, s_gh, s_gl, s_dn, s_y, s_meta = (sem(v) for v in
            ("xtr", "xh", "xl", "up", "g_ready", "gtr", "gh", "gl", "down", "y", "meta"))
        s_ylow = sem("y_low_ready")
        s_yl = [sem(f"yl{c}") for c in range(CH)]
        s_sum, s_fin, s_out = sem("sum"), sem("fin"), sem("stored")

        block = stack.enter_context(nc.Block())
        K = UNITS * L
        STEPS = K + 8

        def pidx(k):
            l, j = k // UNITS, k % UNITS
            return j // 2 if l == 0 else CH + UNITS * (l - 1) + j

        def unit_of(p):
            return 2 * p + 1 if p < CH else p + CH

        def projects(s):
            return s < K and (s >= UNITS or s % 2 == 0)

        def staged(i):
            return wst[:, i % 2].rearrange("p (f c) -> p f c", f=FC)

        def split_part(i, part):
            return w1s[:, i // 2, part].rearrange("p (f c) -> p f c", f=FC) if i % 2 == 0 else w2s[:, i // 2, :, part]

        def block_steps(engine, step):
            for s in range(Q):
                step(s, s)
            with engine.Fori(1, BLK // Q) as i:
                for u in range(Q):
                    step(i * Q + u, u)
            for s in range(BLK, BLK + 3):
                step(s, s % Q)

        def has(s, d):
            return not isinstance(s, int) or 0 <= s - d < BLK

        @block.sync
        def _(sp):
            xv = x.rearrange("b s d -> s b d")
            sp.dma_start(xt[:, 0:TPC, :], xv[:, 0:TPC, :]).then_inc(s_ldx[0], 16)
            sp.dma_start(w_raw[:], ctx_w[0:L].rearrange("l h i -> h l i")).then_inc(s_ldw, 16)
            for c in range(1, CH):
                sp.dma_start(xt[:, c * TPC:(c + 1) * TPC, :], xv[:, c * TPC:(c + 1) * TPC, :]).then_inc(s_ldx[c], 16)
            for i in range(2 * E):
                after(sp, s_split, i - 1)
                e = i // 2
                if i % 2 == 0:
                    sp.dma_start(wst[:, 0, :], w1[e]).then_inc(s_lde[0], 16)
                else:
                    sp.dma_start(wst[:, 1, :].rearrange("p (f c) -> p f c", f=FC),
                                 w2[e].rearrange("(f p) c -> p f c", p=P)).then_inc(s_lde[1], 16)
                if i == 2:
                    sp.wait_ge(s_padw, 1)
                    sp.dma_start(rows[E * REG:E * REG + DUMMY * P, :].rearrange("(b p) c -> p b c", p=P),
                                 pad[:, E:E + DUMMY, :]).then_inc(s_pads, 16)
            sp.wait_ge(s_tab, 1)
            for e in range(0, E, 2):
                at = sp.value_load(prow[0:1, e:e + 1], min_val=0, max_val=E * REG)
                sp.dma_start(rows[bass.ds(at, P), :], pad[:, e, :]).then_inc(s_pads, 16)
            sp.wait_ge(s_scat, 16 * 2 * B)
            sp.wait_ge(s_pads, 16 * (E + 1))
            sp.wait_ge(s_tab, 2)

            def load(j, q):
                after(sp, s_meta, j - Q + 1)
                at = sp.value_load(brow[0:1, bass.ds(j, 1)], min_val=0, max_val=E * REG + (DUMMY - 1) * P)
                sp.dma_start(xb[:, q, :], rows[bass.ds(at, P), :]).then_inc(s_xb[q], 16)

            for j in range(Q):
                load(j, j)
            with sp.Fori(1, BLK // Q) as i:
                for u in range(Q):
                    load(i * Q + u, u)
            for q in range(Q):
                sp.wait_ge(s_sc[q], 16 * (BLK // Q))
            for c in range(CH):
                sp.dma_start(yall[:, c], yrows[c * 2 * N:(c + 1) * 2 * N, :].rearrange("(t p k) h -> p t k h", p=P, k=2)
                             ).then_inc(s_yl[c], 16)
            for c in range(CH):
                sp.wait_ge(s_fin, c + 1)
                sp.dma_start(out.rearrange("b s d -> s b d")[:, c * TPC:(c + 1) * TPC, :],
                             x2[:, c * TPC:(c + 1) * TPC, :]).then_inc(s_out, 16)
            sp.wait_ge(s_out, 16 * CH)

        @block.scalar
        def _(act):
            act.dma_start(gam[:], ln_gamma.rearrange("(p o) -> p o", o=1)).then_inc(s_ldc, 16)
            act.dma_start(bet[:], ln_beta.rearrange("(p o) -> p o", o=1)).then_inc(s_ldc, 16)
            act.dma_start(b_rows[:], cond[0:L]).then_inc(s_ldc, 16)
            act.dma_start(fw_raw[:], fusion_w.rearrange("o (d i) -> o d i", d=2)).then_inc(s_ldf, 16)
            act.dma_start(fb_row[:], fusion_b.rearrange("(o p) -> o p", o=1)).then_inc(s_ldf, 16)
            act.dma_start(gw[:], gate_w).then_inc(s_ldg, 16)

            def copy_x0T(c):
                act.wait_ge(s_tr, c + 1)
                nc.scalar.copy(x0T[:, c * N:(c + 1) * N], pR[c % 2][:]).then_inc(s_xt, 1)

            def tanhs(k):
                l, p = k // UNITS, pidx(k)
                act.wait_ge(s_u, p + 1)
                if p >= NB:
                    act.wait_ge(s_b, p - NB + 1)
                    act.wait_ge(s_a0, unit_of(p - NB) + 1)
                if p == 0:
                    act.wait_ge(s_wt, 3)
                if p == CH:
                    act.wait_ge(s_wt, 5)
                q = p % NB
                nc.scalar.activation(T1[:, q], pU[p % 2][:], ACT.Tanh, bias=b_full[:, l:l + 1]).then_inc(s_t, 1)
                nc.scalar.activation(T2[:, q], pU[p % 2][:], ACT.Tanh, bias=b_half[:, l:l + 1], scale=-0.5).then_inc(s_t, 1)

            def centre(k):
                l = k // UNITS
                act.wait_ge(s_c, k + 1)
                after(act, s_n, k - NB + 1)
                after(act, s_v, k - NB + 1)
                q = k % NB
                nc.scalar.activation(SQ[:, q], pC[k % 2][:], ACT.Square, bias=cb[:, l:l + 1]).then_inc(s_sq, 1)
                nc.scalar.activation(CS[:, q], pC[k % 2][:], ACT.Identity, bias=cb[:, l:l + 1]).then_inc(s_cs, 1)

            def split_high(i):
                act.wait_ge(s_lde[i % 2], 16 * (i // 2 + 1))
                nc.scalar.activation(split_part(i, 0), staged(i), ACT.Copy).then_inc(s_high, 1)

            def post_transposed(c):
                act.wait_ge(s_xn, c + 1)
                tiles = slice(c * TPC, (c + 1) * TPC)
                nc.scalar.copy(xr[:, 1, tiles, 0:H], xr[:, 0, tiles, 0:H]).then_inc(s_xr, 1)
                act.wait_ge(s_tr2, c + 1)
                nc.scalar.copy(x0T[:, c * N:(c + 1) * N], post_bank[c][:]).then_inc(s_xt2, 1)

            def post_exp(c):
                act.wait_ge(s_sub, c + 1)
                nc.scalar.activation(pr[:], t8[:], ACT.Exp).then_inc(s_exp, 1)

            copy_x0T(0)
            act.wait_ge(s_pool, 5)
            for s in range(STEPS):
                if 1 <= s < CH:
                    copy_x0T(s)
                if projects(s):
                    tanhs(s)
                if 0 <= s - 2 < K:
                    centre(s - 2)
                if 6 <= s < 6 + 2 * E:
                    split_high(s - 6)
                for c in range(CH):
                    if s == 31 + 2 * c:
                        post_transposed(c)
                    if s == 32 + 2 * c:
                        post_exp(c)
            act.wait_ge(s_tab, 1)
            for e in range(1, E, 2):
                at = act.value_load(prow[0:1, e:e + 1], min_val=0, max_val=E * REG)
                act.dma_start(rows[bass.ds(at, P), :], pad[:, e, :]).then_inc(s_pads, 16)

            def step(s, u):
                if has(s, 0):
                    act.wait_ge(s_xtr, s + 1)
                    after(act, s_up, s - 1)
                    nc.scalar.activation(xh[:, u % 2], banks[u % 2][:, 0:P], ACT.Copy).then_inc(s_xh, 1)
                if has(s, 1):
                    act.wait_ge(s_up, s)
                    after(act, s_gtr, s - 2)
                    nc.scalar.activation(g[:, (u - 1) % 2], banks[2 + (u - 1) % 2][:], ACT.Gelu).then_inc(s_g, 1)
                if has(s, 2):
                    act.wait_ge(s_gtr, s - 1)
                    after(act, s_dn, s - 3)
                    nc.scalar.activation(gh[:, u % 2], banks[4 + u % 2][:], ACT.Copy).then_inc(s_gh, 1)
                if has(s, 3):
                    q = (u - 3) % 2
                    act.wait_ge(s_dn, s - 2)
                    act.wait_ge(s_meta, s - 2)
                    after(act, s_y, s - 4)
                    nc.scalar.activation(yl[:, q], banks[6 + q][:, H:2 * H], ACT.Copy, scale=meta[:, (u - 3) % Q, 1:2]
                                         ).then_inc(s_ylow, 1)

            block_steps(act, step)

        @block.gpsimd
        def _(pool):
            nc.gpsimd.memset(ident[:], 0.0).then_inc(s_pool, 1)
            nc.gpsimd.memset(mhalf[:], -0.5).then_inc(s_pool, 1)
            nc.gpsimd.memset(inv_h[:], 1.0 / H).then_inc(s_pool, 1)
            nc.gpsimd.memset(ones_row[:], 1.0).then_inc(s_pool, 1)
            nc.gpsimd.memset(cb[:], 0.0).then_inc(s_pool, 1)
            pool.wait_ge(s_pool, 5)
            nc.gpsimd.affine_select(out=ident[:], in_=ident[:], compare_op=ALU.not_equal, fill=1.0, base=0,
                                    pattern=[[-1, P]], channel_multiplier=1).then_inc(s_const, 1)

            def power0(c, count, counted):
                pool.wait_ge(counted, count)
                nc.gpsimd.tensor_tensor(rs0[:, c * TPC:(c + 1) * TPC], vpe[:, c * TPC:(c + 1) * TPC],
                                        mhalf[:], ALU.pow).then_inc(s_rs0, 1)

            power0(0, 1, s_st)
            nc.gpsimd.memset(ones_bf[:], 1.0).then_inc(s_pool, 1)
            nc.gpsimd.memset(Mc[:, 0], 0.0).then_inc(s_pool, 1)
            nc.gpsimd.memset(ones8[:], 1.0).then_inc(s_pool, 1)
            nc.gpsimd.memset(pad[:], 0.0).then_inc(s_pool, 1)
            pool.wait_ge(s_pool, 9)
            nc.gpsimd.affine_select(out=before[:], in_=ones_bf[:], compare_op=ALU.is_gt, fill=0.0, base=0,
                                    pattern=[[1, P]], channel_multiplier=-1).then_inc(s_const, 1)
            loose = dict(allow_small_or_imprecise_dtypes=True)
            nc.gpsimd.iota(rank[:], pattern=[[0, TPC], [-1, E]], base=E, channel_multiplier=0, **loose).then_inc(s_const, 1)
            nc.gpsimd.iota(eoff[:], pattern=[[0, TPC], [REG, E]], base=0, channel_multiplier=0, **loose).then_inc(s_const, 1)
            nc.gpsimd.iota(c128[:], pattern=[[0, E], [P, B]], base=0, channel_multiplier=0, **loose).then_inc(s_const, 1)
            nc.gpsimd.iota(jj[:], pattern=[[1, BLK], [0, E]], base=0, channel_multiplier=0, **loose).then_inc(s_const, 1)
            for k in range(2):
                nc.gpsimd.iota(xr[:, k, :, DEST].bitcast(U32), pattern=[[2 * P, B]], base=k, channel_multiplier=2
                               ).then_inc(s_const, 1)
            nc.gpsimd.iota(pad[:, :, DEST].bitcast(U32), pattern=[[P, E + DUMMY]], base=2 * B * P, channel_multiplier=1
                           ).then_inc(s_padw, 1)

            def decay(k):
                p = pidx(k)
                pool.wait_ge(s_t, 2 * p + 2)
                after(pool, s_r, k - NB + 1)
                nc.gpsimd.tensor_scalar(Ab[:, k % NB], T2[:, p % NB], 0.5, 0.5, ALU.mult, ALU.add).then_inc(s_a0, 1)

            def power(k):
                pool.wait_ge(s_ve, k + 1)
                after(pool, s_rb, k - NB + 1)
                nc.gpsimd.tensor_tensor(rs[:, k % NB], ve[:, k % NB], mhalf[:], ALU.pow).then_inc(s_p, 1)

            def split(i):
                pool.wait_ge(s_high, i + 1)
                nc.gpsimd.tensor_tensor(split_part(i, 1), staged(i), split_part(i, 0).bitcast(F32), ALU.subtract
                                        ).then_inc(s_split, 1)

            for s in range(STEPS):
                if s < K:
                    decay(s)
                if 0 <= s - 3 < K:
                    power(s - 3)
                if s < CH - 1:
                    power0(s + 1, s + 2, s_st)
                if 6 <= s < 6 + 2 * E:
                    split(s - 6)
                for c in range(CH):
                    if s == 30 + 2 * c:
                        power0(c, c + 1, s_st2)
                    if s == 33 + 2 * c:
                        pool.wait_ge(s_slot, c + 1)
                        pool.wait_ge(s_xr, c + 1)
                        for k in range(2):
                            for t in range(TPC):
                                nc.gpsimd.indirect_dma_start(
                                    rows[:], bass.IndirectOffsetOnAxis(slot[:, c, k, t:t + 1], 0),
                                    xr[:, k, c * TPC + t, :], None).then_inc(s_scat, 16)

            for j in range(BLK):
                q = j % Q
                pool.wait_ge(s_y, j + 1)
                nc.gpsimd.indirect_dma_start(yrows[:], bass.IndirectOffsetOnAxis(meta[:, q, 0:1].bitcast(U32), 0),
                                             yb[:, q, :], None).then_inc(s_sc[q], 16)

        @block.vector
        def _(dve):
            steps = [0]

            def done(ins):
                steps[0] += 1
                ins.then_inc(s_dve, 1)

            def link(ins):
                done(ins)
                dve.wait_ge(s_dve, steps[0])

            def layernorm(src, c):
                for t in range(c * TPC, (c + 1) * TPC):
                    done(nc.vector.bn_stats(stats[:, t], src[:, t]))
                dve.wait_ge(s_dve, steps[0])
                for t in range(c * TPC, (c + 1) * TPC):
                    done(nc.vector.bn_aggr(mv[:, t], stats[:, t]))
                dve.wait_ge(s_dve, steps[0])
                return nc.vector.tensor_scalar(vpe[:, c * TPC:(c + 1) * TPC], mv[:, c * TPC:(c + 1) * TPC, 1], LN_EPS,
                                               None, ALU.add)

            def normed(dst, src, c, count):
                dve.wait_ge(s_rs0, count)
                for t in range(c * TPC, (c + 1) * TPC):
                    ins = nc.vector.tensor_scalar(dst(t), src[:, t], mv[:, t, 0:1], rs0[:, t:t + 1],
                                                  ALU.subtract, ALU.mult)
                return ins

            def drive(k):
                p = pidx(k)
                dve.wait_ge(s_t, 2 * p + 2)
                q = p % NB
                nc.vector.scalar_tensor_tensor(out=Bb[:, q], in0=T2[:, q], scalar=-1.0, in1=T1[:, q],
                                               op0=ALU.add, op1=ALU.mult).then_inc(s_b, 1)

            def clip(k):
                q = k % NB
                dve.wait_ge(s_a0, k + 1)
                link(nc.vector.tensor_scalar(Ab[:, q], Ab[:, q], CLAMP_LO, CLAMP_HI, ALU.max, ALU.min))
                first = 0 if k % 2 == 0 else P - 1
                nc.vector.memset(Ab[:, q, first::P], 0.0).then_inc(s_a, 1)

            def scan(k):
                l, j, p = k // UNITS, k % UNITS, pidx(k)
                dve.wait_ge(s_b, p + 1)
                dve.wait_ge(s_a, k + 1)
                after(dve, s_c, k - NB + 1)
                q, d, c = k % NB, j % 2, j // 2
                way = slice(None) if d == 0 else slice(None, None, -1)
                a_, b_, o_ = (v[:, way] for v in (Ab[:, q], Bb[:, p % NB], R[:, q]))
                ins = nc.vector.tensor_tensor_scan(out=o_, data0=a_, data1=b_, initial=0.0, op0=ALU.mult, op1=ALU.add)
                if l == 0:
                    ins.then_inc(s_r, 1)
                    return
                ins.then_inc(s_s, 1)
                dve.wait_ge(s_s, k - UNITS + 1)
                nc.vector.scalar_tensor_tensor(out=R[:, q], in0=n[:, d, c * N:(c + 1) * N], scalar=gam2[:],
                                               in1=R[:, q], op0=ALU.mult, op1=ALU.add).then_inc(s_r, 1)

            def addeps(k):
                dve.wait_ge(s_v, k + 1)
                after(dve, s_p, k - NB + 1)
                nc.vector.tensor_scalar(ve[:, k % NB], pV[:, 0:TPC], 4 * LN_EPS, None, ALU.add).then_inc(s_ve, 1)

            def norm(k):
                j = k % UNITS
                q, d, c = k % NB, j % 2, j // 2
                dve.wait_ge(s_rb, k + 1)
                dve.wait_ge(s_cs, k + 1)
                nc.vector.tensor_tensor(n[:, d, c * N:(c + 1) * N], CS[:, q], pR[k % 2][:], ALU.mult).then_inc(s_n, 1)

            def col(v, m=TPC):
                return v[:].unsqueeze(2).to_broadcast([P, m, E])

            def post_x2(c):
                tiles = slice(c * TPC, (c + 1) * TPC)
                dve.wait_ge(s_f, c + 1)
                nc.vector.tensor_tensor(x2[:, tiles], xt[:, tiles], post_bank[c][:].rearrange("p (t h) -> p t h", t=TPC),
                                        ALU.add).then_inc(s_x2, 1)
                dve.wait_ge(s_x2, c + 1)
                layernorm(x2, c).then_inc(s_st2, 1)

            def post_route(c):
                tiles = slice(c * TPC, (c + 1) * TPC)
                dve.wait_ge(s_lg, c + 1)
                lg = post_bank[c][:, 0:TPC * E].rearrange("p (t e) -> p t e", e=E)
                link(nc.vector.tensor_reduce(mx[:], lg, AX_X, ALU.max))
                nc.vector.tensor_tensor(t8[:], lg, col(mx), ALU.subtract).then_inc(s_sub, 1)
                dve.wait_ge(s_exp, c + 1)
                link(nc.vector.tensor_reduce(mx[:], pr[:], AX_X, ALU.add))
                link(nc.vector.reciprocal(mx[:], mx[:]))
                link(nc.vector.tensor_tensor(pr[:], pr[:], col(mx), ALU.mult))
                for k in range(2):
                    link(nc.vector.tensor_reduce(mk[k][:], pr[:], AX_X, ALU.max))
                    link(nc.vector.tensor_tensor(t8[:], pr[:], col(mk[k]), ALU.is_equal))
                    link(nc.vector.tensor_tensor(cand[:], t8[:], rank[:], ALU.mult))
                    link(nc.vector.tensor_reduce(mx[:], cand[:], AX_X, ALU.max))
                    link(nc.vector.tensor_tensor(oh[k][:], cand[:], col(mx), ALU.is_equal))
                    if k == 0:
                        link(nc.vector.scalar_tensor_tensor(out=pr[:], in0=oh[0][:], scalar=-2.0, in1=pr[:],
                                                            op0=ALU.mult, op1=ALU.add))
                link(nc.vector.tensor_tensor(M[:, tiles], oh[0][:], oh[1][:], ALU.add))
                for t in range(c * TPC, (c + 1) * TPC):
                    ins = nc.vector.tensor_tensor(Mc[:, t + 1], Mc[:, t], M[:, t], ALU.add)
                    if t == (c + 1) * TPC - 1:
                        done(ins)
                        ins = None
                    else:
                        link(ins)
                link(nc.vector.tensor_tensor(mx[:], mk[0][:], mk[1][:], ALU.add))
                nc.vector.reciprocal(mx[:], mx[:]).then_inc(s_m, 1)
                dve.wait_ge(s_m, c + 1)
                for k in range(2):
                    done(nc.vector.tensor_tensor(xr[:, k, tiles, WGT], mk[k][:], mx[:], ALU.mult))

            def post_slots(c):
                dve.wait_ge(s_pos, c + 1)
                pos = post_bank[c][:, 0:TPC * E].rearrange("p (t e) -> p t e", e=E)
                link(nc.vector.tensor_tensor(t8[:], pos, eoff[:], ALU.add))
                for k in range(2):
                    link(nc.vector.tensor_tensor(cand[:], t8[:], oh[k][:], ALU.mult))
                    link(nc.vector.tensor_reduce(slotf[:, k], cand[:], AX_X, ALU.add))
                nc.vector.tensor_copy(slot[:, c], slotf[:]).then_inc(s_slot, 1)

            dve.wait_ge(s_ldx[0], 16)
            layernorm(xt, 0).then_inc(s_st, 1)
            dve.wait_ge(s_ldc, 48)
            dve.wait_ge(s_const, 1)
            done(nc.vector.tensor_scalar(ngam[:], gam[:], -1.0, None, ALU.mult))
            done(nc.vector.tensor_scalar(gam2[:], gam[:], 2.0, None, ALU.mult))
            nc.vector.tensor_scalar(cmat[:], ident[:], -1.0 / H, None, ALU.add).then_inc(s_wt, 1)
            normed(lambda t: x0[:, t], xt, 0, 1).then_inc(s_x0, 1)
            dve.wait_ge(s_prep, 1)
            link(nc.vector.tensor_copy(b_full[:, 0:1], pV[:, 0:1]))
            done(nc.vector.tensor_copy(b_raw[:], pV[:, 0:L]))
            nc.vector.tensor_scalar(b_half[:, 0:1], b_full[:, 0:1], -0.5, None, ALU.mult).then_inc(s_wt, 1)
            dve.wait_ge(s_prep, 2)
            nc.vector.tensor_copy(wt_raw[:], pX[:]).then_inc(s_wt, 1)

            for s in range(STEPS):
                if 0 <= s - 1 < K:
                    clip(s - 1)
                    scan(s - 1)
                if projects(s):
                    drive(s)
                if 0 <= s - 3 < K:
                    addeps(s - 3)
                if 0 <= s - 4 < K:
                    norm(s - 4)
                if s < CH - 1:
                    dve.wait_ge(s_ldx[s + 1], 16)
                    layernorm(xt, s + 1).then_inc(s_st, 1)
                    normed(lambda t: x0[:, t], xt, s + 1, s + 2).then_inc(s_x0, 1)
                if s == 0:
                    link(nc.vector.tensor_scalar(wt_g[:], wt_raw[:], ngam[:], None, ALU.mult))
                if s == 3:
                    dve.wait_ge(s_prep, 3)
                    link(nc.vector.tensor_copy(fwt_raw[:], pX[:, 0:2 * H].rearrange("p (d o) -> p d o", d=2)))
                    nc.vector.tensor_scalar(fwt_g[:], fwt_raw[:], ngam[:], None, ALU.mult).then_inc(s_wt, 1)
                if s == 4:
                    dve.wait_ge(s_prep, 4)
                    done(nc.vector.tensor_scalar(cb[:, 1:L], pX[:, L:L + 1].to_broadcast([P, L - 1]), -2.0, None, ALU.mult))
                    link(nc.vector.tensor_tensor(b_full[:, 1:L], pX[:, 1:L], b_raw[:, 1:L], ALU.add))
                    nc.vector.tensor_scalar(b_half[:, 1:L], b_full[:, 1:L], -0.5, None, ALU.mult).then_inc(s_wt, 1)
                if s == 5:
                    dve.wait_ge(s_prep, 5)
                    link(nc.vector.tensor_copy(fbias[:], pX[:, 0:H]))
                if 6 <= s < 6 + CH:
                    tiles = slice((s - 6) * TPC, (s - 5) * TPC)
                    done(nc.vector.tensor_tensor(xt[:, tiles], xt[:, tiles],
                                                 fbias[:].unsqueeze(1).to_broadcast([P, TPC, H]), ALU.add))
                if s == 12:
                    dve.wait_ge(s_const, 8)
                for c in range(CH):
                    if s == 30 + 2 * c:
                        post_x2(c)
                    if s == 31 + 2 * c:
                        normed(lambda t: xr[:, 0, t, 0:H], x2, c, CH + c + 1).then_inc(s_xn, 1)
                    if s == 32 + 2 * c:
                        post_route(c)
                    if s == 33 + 2 * c:
                        post_slots(c)

            dve.wait_ge(s_cnt, 1)
            link(nc.vector.tensor_copy(cnt[:], post_bank[0][0:1, 0:E]))
            nc.vector.tensor_tensor(prow[:], cnt[:], eoff[0:1, 0], ALU.add).then_inc(s_tab, 1)
            link(nc.vector.tensor_tensor(gtc[:], cnt[:].unsqueeze(2).to_broadcast([1, E, B]), c128[:], ALU.is_gt))
            link(nc.vector.tensor_reduce(nblk[:], gtc[:], AX_X, ALU.add))
            done(nc.vector.tensor_scalar(dlt[:], nblk[:], -float(P), float(REG), ALU.mult, ALU.add))
            link(nc.vector.tensor_tensor_scan(out=endb[:], data0=ones8[:], data1=nblk[:], initial=0.0,
                                              op0=ALU.mult, op1=ALU.add))
            link(nc.vector.tensor_tensor(ge[:], jj[:], endb[:].unsqueeze(1).to_broadcast([1, BLK, E]), ALU.is_ge))
            link(nc.vector.tensor_reduce(tj[:], ge[:], AX_X, ALU.add))
            done(nc.vector.tensor_scalar(eid[:], tj[:], float(E - 1), None, ALU.min))
            link(nc.vector.tensor_tensor(ge[:], ge[:], dlt[:].unsqueeze(1).to_broadcast([1, BLK, E]), ALU.mult))
            link(nc.vector.tensor_reduce(tr_[:], ge[:], AX_X, ALU.add))
            nc.vector.scalar_tensor_tensor(out=brow[:], in0=jj[:, :, 0], scalar=float(P), in1=tr_[:],
                                           op0=ALU.mult, op1=ALU.add).then_inc(s_tab, 1)

            def step(s, u):
                if has(s, 0):
                    dve.wait_ge(s_xh, s + 1)
                    nc.vector.tensor_tensor(xl[:, u % 2], banks[u % 2][:, 0:P], xh[:, u % 2].bitcast(F32),
                                            ALU.subtract).then_inc(s_xl, 1)
                    if not isinstance(s, int):
                        dve.wait_ge(s_sc[u], (16 // Q) * (s - u))
                    nc.vector.tensor_copy(meta[:, u], xb[:, u, H:RW]).then_inc(s_meta, 1)
                if has(s, 2):
                    dve.wait_ge(s_gh, s - 1)
                    nc.vector.tensor_tensor(gl[:, u % 2], banks[4 + u % 2][:], gh[:, u % 2].bitcast(F32),
                                            ALU.subtract).then_inc(s_gl, 1)
                if has(s, 3):
                    q = (u - 3) % Q
                    dve.wait_ge(s_ylow, s - 2)
                    nc.vector.scalar_tensor_tensor(out=yb[:, q], in0=banks[6 + (u - 3) % 2][:, 0:H],
                                                   scalar=meta[:, q, 1:2], in1=yl[:, (u - 3) % 2],
                                                   op0=ALU.mult, op1=ALU.add).then_inc(s_y, 1)

            block_steps(dve, step)
            for c in range(CH):
                tiles = slice(c * TPC, (c + 1) * TPC)
                dve.wait_ge(s_yl[c], 16)
                nc.vector.tensor_tensor(x2[:, tiles], x2[:, tiles], yall[:, c, :, 0], ALU.add).then_inc(s_sum, 1)
                dve.wait_ge(s_sum, c + 1)
                nc.vector.tensor_tensor(x2[:, tiles], x2[:, tiles], yall[:, c, :, 1], ALU.add).then_inc(s_fin, 1)

        @block.tensor
        def _(pe):
            mm, tr = nc.tensor.matmul, nc.tensor.transpose

            def transpose_x0(c):
                pe.wait_ge(s_x0, c + 1)
                after(pe, s_xt, c - 1)
                for t in range(TPC):
                    ins = tr(pR[c % 2][:, t * P:(t + 1) * P], x0[:, c * TPC + t, :], ident[:])
                ins.then_inc(s_tr, 1)

            pe.wait_ge(s_const, 1)
            pe.wait_ge(s_ldc, 48)
            mm(pV[:, 0:L], b_rows[:], ident[0:L, 0:L], start=True, stop=True).then_inc(s_prep, 1)
            pe.wait_ge(s_ldw, 16)
            for l in range(L):
                ins = tr(pX[:, l * H:(l + 1) * H], w_raw[:, l, :], ident[:])
            ins.then_inc(s_prep, 1)
            transpose_x0(0)

            def project(k):
                l, j, p = k // UNITS, k % UNITS, pidx(k)
                d, c = j % 2, j // 2
                if l == 0:
                    pe.wait_ge(s_xt, c + 1)
                    src, wt = x0T[:, c * N:(c + 1) * N], wt_raw
                else:
                    pe.wait_ge(s_n, k - UNITS + 1)
                    src, wt = n[:, d, c * N:(c + 1) * N], wt_g
                after(pe, s_t, 2 * (p - 1))
                if k == 0:
                    pe.wait_ge(s_wt, 3)
                mm(pU[p % 2][:], wt[:, l * H:(l + 1) * H], src, start=True, stop=True).then_inc(s_u, 1)

            def centre(k):
                pe.wait_ge(s_r, k + 1)
                after(pe, s_cs, k - 1)
                mm(pC[k % 2][:], cmat[:], R[:, k % NB], start=True, stop=True).then_inc(s_c, 1)

            def variance(k):
                pe.wait_ge(s_sq, k + 1)
                after(pe, s_ve, k)
                for t in range(TPC):
                    ins = mm(pV[:, t:t + 1], SQ[:, k % NB, t * P:(t + 1) * P], inv_h[:], start=True, stop=True)
                ins.then_inc(s_v, 1)

            def spread(k):
                pe.wait_ge(s_p, k + 1)
                after(pe, s_n, k - 1)
                if k == 0:
                    pe.wait_ge(s_xt, CH)
                for t in range(TPC):
                    ins = mm(pR[k % 2][:, t * P:(t + 1) * P], rs[:, k % NB, t:t + 1].to_broadcast([P, P]), ident[:],
                             start=True, stop=True)
                ins.then_inc(s_rb, 1)

            def fuse(c):
                pe.wait_ge(s_n, 3 * UNITS + 2 * c + 2)
                if c == 0:
                    pe.wait_ge(s_prep, 5)
                if c % 2:
                    pe.wait_ge(s_t, 2 * (K - CH))
                if c == 2:
                    pe.wait_ge(s_slot, 1)
                for t in range(TPC):
                    for d in range(2):
                        ins = mm(post_bank[c][:, t * H:(t + 1) * H], n[:, d, (c * TPC + t) * P:(c * TPC + t + 1) * P],
                                 fwt_g[:, d, :], start=(d == 0), stop=(d == 1))
                ins.then_inc(s_f, 1)

            def post_transpose(c):
                pe.wait_ge(s_xn, c + 1)
                for t in range(TPC):
                    ins = tr(post_bank[c][:, t * P:(t + 1) * P], xr[:, 0, c * TPC + t, 0:H], ident[:])
                ins.then_inc(s_tr2, 1)

            def post_logits(c):
                pe.wait_ge(s_ldg, 16)
                pe.wait_ge(s_xt2, c + 1)
                for t in range(TPC):
                    ins = mm(post_bank[c][:, t * E:(t + 1) * E], x0T[:, (c * TPC + t) * P:(c * TPC + t + 1) * P], gw[:],
                             start=True, stop=True)
                ins.then_inc(s_lg, 1)

            def post_positions(c):
                pe.wait_ge(s_const, 2)
                pe.wait_ge(s_m, c + 1)
                tiles = slice(c * TPC, (c + 1) * TPC)
                flat = "p t e -> p (t e)"
                mm(post_bank[c][:, 0:TPC * E], before[:], M[:, tiles].rearrange(flat), start=True, stop=False)
                mm(post_bank[c][:, 0:TPC * E], ones_bf[:], Mc[:, tiles].rearrange(flat), start=False, stop=True
                   ).then_inc(s_pos, 1)

            for s in range(STEPS):
                if projects(s):
                    project(s)
                if 0 <= s - 2 < K:
                    centre(s - 2)
                if 0 <= s - 3 < K:
                    variance(s - 3)
                if 0 <= s - 4 < K:
                    spread(s - 4)
                if 0 <= s < CH - 1:
                    transpose_x0(s + 1)
                if s == 1:
                    pe.wait_ge(s_ldf, 32)
                    for d in range(2):
                        ins = tr(pX[:, d * H:(d + 1) * H], fw_raw[:, d, :], ident[:])
                    ins.then_inc(s_prep, 1)
                if s == 3:
                    pe.wait_ge(s_wt, 4)
                    for l in range(1, L):
                        mm(pX[:, l:l + 1], wt_raw[:, l * H:(l + 1) * H], bet[:], start=True, stop=True)
                    mm(pX[:, L:L + 1], cmat[:], bet[:], start=True, stop=True).then_inc(s_prep, 1)
                if s == 4:
                    pe.wait_ge(s_wt, 5)
                    for d in range(2):
                        mm(pX[:, 0:H], bet[:].to_broadcast([P, P]), fwt_raw[:, d, :], start=(d == 0), stop=False)
                    mm(pX[:, 0:H], ones_row[:], fb_row[:], start=False, stop=True).then_inc(s_prep, 1)
                for c in range(CH):
                    if s == 30 + 2 * c:
                        fuse(c)
                    if s == 31 + 2 * c:
                        post_transpose(c)
                    if s == 32 + 2 * c:
                        post_logits(c)
                    if s == 33 + 2 * c:
                        post_positions(c)
            pe.wait_ge(s_slot, 3)
            mm(post_bank[0][:, 0:E], ones_bf[:], Mc[:, B, :], start=True, stop=True).then_inc(s_cnt, 1)

            pe.wait_ge(s_split, 2 * E)
            pe.wait_ge(s_tab, 2)
            pe.wait_ge(s_slot, 4)

            experts = {}

            def expert(s, u, d):
                if d == 1 or u < 2:
                    experts[(u - d) % Q] = pe.value_load(eid[0:1, bass.ds(s - d, 1)], min_val=0, max_val=E - 1)
                return experts[(u - d) % Q]

            def step(s, u):
                if has(s, 1):
                    e = expert(s, u, 1)
                if has(s, 0):
                    q = u % Q
                    pe.wait_ge(s_xb[q], (16 // Q) * (s - q) + 16)
                    tr(banks[q % 2][:, 0:P], xb[:, q, 0:H], ident[:]).then_inc(s_xtr, 1)
                if has(s, 1):
                    q = (u - 1) % 2
                    pe.wait_ge(s_xl, s)
                    mm(banks[2 + q][:], xh[:, q], w1s[:, :, 0][:, bass.ds(e, 1)], start=True, stop=False)
                    mm(banks[2 + q][:], xh[:, q], w1s[:, :, 1][:, bass.ds(e, 1)], start=False, stop=False)
                    mm(banks[2 + q][:], xl[:, q], w1s[:, :, 0][:, bass.ds(e, 1)], start=False, stop=True).then_inc(s_up, 1)
                if has(s, 3):
                    e = expert(s, u, 3)
                if has(s, 2):
                    q = (u - 2) % 2
                    pe.wait_ge(s_g, s - 1)
                    for f in range(FC):
                        ins = tr(banks[4 + q][:, f * P:(f + 1) * P], g[:, q, f * P:(f + 1) * P], ident[:])
                    ins.then_inc(s_gtr, 1)
                if has(s, 3):
                    q = (u - 3) % 2
                    pe.wait_ge(s_gl, s - 2)
                    after(pe, s_y, s - 4)
                    for f in range(FC):
                        cols = slice(f * P, (f + 1) * P)
                        both = w2s[:, :, f].rearrange("p e k c -> p e (k c)")
                        mm(banks[6 + q][:, 0:2 * H], gh[:, q, cols], both[:, bass.ds(e, 1)], start=(f == 0), stop=False)
                        ins = mm(banks[6 + q][:, 0:H], gl[:, q, cols], both[:, :, 0:H][:, bass.ds(e, 1)],
                                 start=False, stop=(f == FC - 1))
                    ins.then_inc(s_dn, 1)

            block_steps(pe, step)


_INS = ["x", "ctx_1024", "cond_1024", "L0_xcond_fusion_W", "L0_xcond_fusion_b", "L0_xcond_ln_gamma", "L0_xcond_ln_beta",
        "L0_ffn_gate_w", "L0_ffn_w1", "L0_ffn_w2"]


def kernel(**inputs):
    import numpy as np
    import concourse.bacc as bacc
    from concourse.bass_utils import run_bass_kernel_spmd

    nc = bacc.Bacc("TRN2", target_bir_lowering=False, num_devices=1)
    arrays, args = {}, []
    for name in _INS:
        a = np.ascontiguousarray(inputs[name])
        arrays[f"in_{name}"] = a
        args.append(nc.dram_tensor(f"in_{name}", a.shape, mybir.dt.from_np(a.dtype), kind="ExternalInput").ap())
    args.append(nc.dram_tensor("out", (B, P, H), F32, kind="ExternalOutput").ap())
    args.append(nc.dram_tensor("rows", (E * REG + DUMMY * P, RW), F32).ap())
    args.append(nc.dram_tensor("yrows", ((2 * B + E + DUMMY) * P, H), F32).ap())
    program(nc, *args)
    return run_bass_kernel_spmd(nc, [arrays], core_ids=[0]).results[0]["out"]
```

```python
from contextlib import ExitStack

import concourse.bass as bass
from concourse import mybir

ALU = mybir.AluOpType
ACT = mybir.ActivationFunctionType
F32 = mybir.dt.float32
F32R = mybir.dt.float32r
BF16 = mybir.dt.bfloat16
U32 = mybir.dt.uint32
AX_X = mybir.AxisListType.X

P = 128
B = 16
H = 128
CH = 4
TPC = B // CH
N = TPC * P
L = 4
E = 8
F = 512
FC = F // P
NB = 3
BLK = 2 * B + E - 1
DUMMY = BLK - 2 * B
REG = B * P + P
RW = H + 2
DEST, WGT = H, H + 1
Q = 8
LN_EPS = 1e-5
CLAMP_LO = 1e-8
CLAMP_HI = 1.0 - 1e-8

ORDER = [(0, 0), (0, 1), (0, 2), (1, 0), (0, 3), (1, 1), (2, 0), (1, 2), (1, 3), (3, 0), (2, 1), (2, 2), (2, 3),
         (3, 1), (3, 2), (3, 3)]
POST = dict(fuse=(12, 12, 10, 10), x2=(12, 12, 10, 12), stats=(13, 13, 12, 13), rstd=(13, 14, 15, 15),
            normed=(16, 14, 16, 15), turn=(18, 16, 17, 17), turned=(19, 16, 17, 17), logits=(20, 18, 18, 18),
            route=(21, 18, 18, 18), exp=(22, 18, 18, 18), positions=(22, 19, 19, 19), slots=(22, 20, 20, 20),
            scatter=(23, 22, 22, 22))


def after(engine, semaphore, count):
    if not (isinstance(count, int) and count <= 0):
        engine.wait_ge(semaphore, count)


def program(nc, x, ctx_w, cond, fusion_w, fusion_b, ln_gamma, ln_beta, gate_w, w1, w2, out, rows, yrows):
    with ExitStack() as stack:
        def sb(name, shape, dt=F32):
            return stack.enter_context(nc.sbuf_tensor(name, shape, dt))

        def sem(name):
            return stack.enter_context(nc.semaphore(name))

        banks = [stack.enter_context(nc.psum_tensor(f"bank{i}", [P, 512], F32)) for i in range(8)]
        pU, pC, pR = banks[0:2], banks[2:4], banks[6:8]
        pV, pX = banks[4], banks[5]
        post_bank = [pX, pU[0], pX, pU[1]]

        xt = sb("x_tokens", [P, B, H])
        x2 = sb("x2", [P, B, H])
        x0 = x2
        x0T = sb("x_normed_T", [P, CH * N])
        ident = sb("ident", [P, P])
        cmat = sb("centering", [P, P])
        before = sb("tokens_before", [P, P], BF16)
        ones_bf = sb("ones_bf", [P, P], BF16)
        inv_h = sb("inv_h", [P, 1])
        ones_row = sb("ones_row", [1, P])
        w_raw = sb("w_raw", [P, L, H])
        wt_raw = sb("wt_raw", [P, L * H])
        wt_g = sb("wt_g", [P, L * H])
        gam = sb("gamma", [P, 1])
        bet = sb("beta", [P, 1])
        ngam = sb("neg_gamma", [P, 1])
        gam2 = sb("two_gamma", [P, 1])
        b_rows = sb("b_rows", [L, H])
        b_raw = sb("b_raw", [P, L])
        b_full = sb("b_full", [P, L])
        b_half = sb("b_neg_half", [P, L])
        cb = sb("centered_beta", [P, L])
        fw_raw = sb("fw_raw", [P, 2, H])
        fwt_raw = sb("fwt_raw", [P, 2, H])
        fwt_g = sb("fwt_g", [P, 2, H])
        fb_row = sb("fb_row", [1, H])
        fbias = sb("fbias", [P, H])
        gw = sb("gate_w", [P, E])
        wst = sb("w_stage", [P, 2, F])
        w1s = sb("w1_split", [P, E, 2, F], F32R)
        w2s = sb("w2_split", [P, E, FC, 2, P], F32R)
        stats = sb("stats", [P, B, 6])
        mv = sb("mv", [P, B, 2])
        vpe = sb("vpe", [P, B])
        rs0 = sb("rs0", [P, B])
        negmu = sb("neg_mean", [P, CH, TPC])
        nm = sb("scaled_mean", [P, CH, TPC])
        mhalf = sb("minus_half", [P, TPC])
        warm = sb("table_warm_up", [P, 1])

        T1 = sb("tanh_u", [P, NB, N])
        T2 = sb("tanh_mhalf_u", [P, NB, N])
        Ab = sb("decay", [P, NB, N])
        Bb = sb("drive", [P, NB, N])
        R = sb("resid", [P, NB, N])
        CS = sb("cent", [P, NB, N])
        SQ = sb("sq", [P, NB, N])
        ve = sb("var_eps", [P, NB, TPC])
        rs = sb("rstd", [P, NB, TPC])
        n = sb("n", [P, 2, CH * N])
        yall = n[:].rearrange("p d (c t) -> p (d c t)", c=CH).rearrange("p (c t k h) -> p c t k h", c=CH, t=TPC, k=2)

        xr = sb("routed_rows", [P, 2, B, RW])
        pad = sb("pad_rows", [P, E + DUMMY, RW])
        top8 = sb("sorted_logits", [P, TPC, E])
        tied = sb("tied", [P, 2, TPC, E])
        best = sb("best_rank", [P, 2, TPC])
        oh = sb("one_hot", [P, 2, TPC, E])
        place = sb("row_of_expert", [P, TPC, E])
        picked = sb("picked", [P, 2, TPC, E])
        rank = sb("rank", [P, 2, TPC, E])
        eoff = sb("expert_start", [P, TPC, E])
        gap = sb("logit_gap", [P, TPC])
        ratio = sb("weight_ratio", [P, TPC])
        total = sb("weight_total", [P, TPC])
        M = sb("chosen", [P, B, E], BF16)
        Msum = sb("chosen_in_chunk", [P, CH, E], BF16)
        slot = sb("slot", [P, CH, 2, TPC], U32)
        cnt = sb("expert_count", [1, E])
        c128 = sb("block_start", [1, E, B])
        gtc = sb("block_used", [1, E, B])
        nblk = sb("blocks_of_expert", [1, E])
        ones8 = sb("ones8", [1, E])
        endb = sb("last_block_end", [1, E])
        dlt = sb("row_step", [1, E])
        jj = sb("block_number", [1, BLK, E])
        ge = sb("past_expert", [1, BLK, E])
        tj = sb("experts_done", [1, BLK])
        tr_ = sb("row_shift", [1, BLK])
        eid = sb("block_expert", [1, BLK], U32)
        brow = sb("block_row", [1, BLK], U32)
        prow = sb("pad_row", [1, E], U32)

        xb = Ab[:].rearrange("p k n -> p (k n)")[:, 0:Q * RW].rearrange("p (q r) -> p q r", q=Q)
        xh, xl = sb("xh", [P, 2, P], F32R), sb("xl", [P, 2, P], F32R)
        g = T1
        gh, gl = sb("gh", [P, 2, F], F32R), sb("gl", [P, 2, F], F32R)
        yl = sb("y_low", [P, 2, H])
        meta = sb("meta", [P, Q, 2])
        yb = T2[:, 0:2, :].rearrange("p t (q h) -> p (t q) h", q=Q // 2)

        w_loaded, columns_loaded, fusion_loaded, gate_loaded = (
            sem(v) for v in ("w_loaded", "columns_loaded", "fusion_loaded", "gate_loaded"))
        x_loaded = [sem(f"x_loaded{c}") for c in range(CH)]
        experts_loaded = [sem(f"experts_loaded{i}") for i in range(2)]
        memsets_done, constants_ready, pads_written = sem("memsets_done"), sem("constants_ready"), sem("pads_written")
        prep_products, prep_copied, wt_ready = sem("prep_products"), sem("prep_copied"), sem("wt_ready")
        high_ready, split_ready = sem("high_ready"), sem("split_ready")
        vector_steps = sem("vector_steps")
        x_stats, token_rstd, x_normed, x_transposed, x_normed_T_ready = (
            sem(v) for v in ("x_stats", "token_rstd", "x_normed", "x_transposed", "x_normed_T_ready"))
        x_biased = sem("x_biased")
        u_ready, tanhs_done, drive_ready = sem("u_ready"), sem("tanhs_done"), sem("drive_ready")
        decay_raw, decay_clipped, decay_ready, scanned, resid_ready = (
            sem(v) for v in ("decay_raw", "decay_clipped", "decay_ready", "scanned", "resid_ready"))
        centred, squared, cent_ready, variance_ready, var_eps_ready = (
            sem(v) for v in ("centred", "squared", "cent_ready", "variance_ready", "var_eps_ready"))
        rstd_ready, rstd_spread, n_ready = sem("rstd_ready"), sem("rstd_spread"), sem("n_ready")
        fused, x2_ready, x2_stats, neg_mean_ready, scaled_mean_ready = (
            sem(v) for v in ("fused", "x2_ready", "x2_stats", "neg_mean_ready", "scaled_mean_ready"))
        x2_normed, second_rows_ready, x2_transposed, x2_normed_T_ready = (
            sem(v) for v in ("x2_normed", "second_rows_ready", "x2_transposed", "x2_normed_T_ready"))
        logits_ready, gap_ready, ratio_ready, weights_ready, chosen_ready, chunk_counted = (
            sem(v) for v in ("logits_ready", "gap_ready", "ratio_ready", "weights_ready", "chosen_ready", "chunk_counted"))
        positions_ready, slots_ready, rows_scattered = (
            sem(v) for v in ("positions_ready", "slots_ready", "rows_scattered"))
        experts_counted, table_ready, pads_stored = (
            sem(v) for v in ("experts_counted", "table_ready", "pads_stored"))
        xb_loaded = [sem(f"xb_loaded{q}") for q in range(Q)]
        y_scattered = [sem(f"y_scattered{q}") for q in range(Q)]
        xb_transposed, xh_ready, xl_ready, meta_ready, up_ready, g_ready = (
            sem(v) for v in ("xb_transposed", "xh_ready", "xl_ready", "meta_ready", "up_ready", "g_ready"))
        g_transposed, gh_ready, gl_ready, down_ready, y_low_ready, y_ready = (
            sem(v) for v in ("g_transposed", "gh_ready", "gl_ready", "down_ready", "y_low_ready", "y_ready"))
        y_loaded = [sem(f"y_loaded{c}") for c in range(CH)]
        first_added, second_added, out_stored = sem("first_added"), sem("second_added"), sem("out_stored")

        block = stack.enter_context(nc.Block())
        K = 2 * len(ORDER)

        def layer(k):
            return ORDER[k // 2][0]

        def chunk(k):
            return ORDER[k // 2][1]

        def unit(l, c, d):
            return 2 * ORDER.index((l, c)) + d

        def below(k):
            return unit(layer(k) - 1, chunk(k), k % 2)

        projected = [k for k in range(K) if layer(k) > 0 or k % 2 == 0]
        upper = [k for k in range(K) if layer(k) > 0]

        def pidx(k):
            return projected.index(k if layer(k) > 0 else k - k % 2)

        def last_unit(p):
            return projected[p] + (layer(projected[p]) == 0)

        def projected_in(s):
            return [k for k in projected if s == (k - 1 if k in (2, 4) else k)]

        def chunks_at(stage, h):
            return [c for c in range(CH) if h == 2 * unit(L - 1, c, 1) + POST[stage][c]]

        STEPS = K + (POST["scatter"][CH - 1] + 2) // 2

        def staged(i):
            return wst[:, i % 2].rearrange("p (f c) -> p f c", f=FC)

        def split_part(i, part):
            return w1s[:, i // 2, part].rearrange("p (f c) -> p f c", f=FC) if i % 2 == 0 else w2s[:, i // 2, :, part]

        def block_steps(engine, step):
            for s in range(Q):
                step(s, s)
            with engine.Fori(1, BLK // Q) as i:
                for u in range(Q):
                    step(i * Q + u, u)
            for s in range(BLK // Q * Q, BLK + 3):
                step(s, s % Q)

        def has(s, d):
            return not isinstance(s, int) or 0 <= s - d < BLK

        @block.sync
        def _(sp):
            xv = x.rearrange("b s d -> s b d")
            sp.dma_start(xt[:, 0:TPC, :], xv[:, 0:TPC, :]).then_inc(x_loaded[0], 16)
            sp.dma_start(w_raw[:], ctx_w[0:L].rearrange("l h i -> h l i")).then_inc(w_loaded, 16)
            for c in range(1, CH):
                sp.dma_start(xt[:, c * TPC:(c + 1) * TPC, :], xv[:, c * TPC:(c + 1) * TPC, :]).then_inc(x_loaded[c], 16)
            for i in range(2 * E):
                after(sp, split_ready, i - 1)
                e = i // 2
                if i % 2 == 0:
                    sp.dma_start(wst[:, 0, :], w1[e]).then_inc(experts_loaded[0], 16)
                else:
                    sp.dma_start(wst[:, 1, :].rearrange("p (f c) -> p f c", f=FC),
                                 w2[e].rearrange("(f p) c -> p f c", p=P)).then_inc(experts_loaded[1], 16)
            sp.wait_ge(pads_written, 1)
            sp.dma_start(rows[E * REG:E * REG + DUMMY * P, :].rearrange("(b p) c -> p b c", p=P),
                         pad[:, E:E + DUMMY, :]).then_inc(pads_stored, 16)
            sp.wait_ge(table_ready, 1)
            for e in range(0, E, 2):
                at = sp.value_load(prow[0:1, e:e + 1], min_val=0, max_val=E * REG)
                sp.dma_start(rows[bass.ds(at, P), :], pad[:, e, :]).then_inc(pads_stored, 16)
            sp.wait_ge(rows_scattered, 16 * 2 * B)
            sp.wait_ge(pads_stored, 16 * (E + 1))
            sp.wait_ge(table_ready, 2)

            def load(j, q):
                after(sp, meta_ready, j - Q + 1)
                at = sp.value_load(brow[0:1, bass.ds(j, 1)], min_val=0, max_val=E * REG + (DUMMY - 1) * P)
                sp.dma_start(xb[:, q, :], rows[bass.ds(at, P), :]).then_inc(xb_loaded[q], 16)

            for j in range(Q):
                load(j, j)
            with sp.Fori(1, BLK // Q) as i:
                for u in range(Q):
                    load(i * Q + u, u)
            for j in range(BLK // Q * Q, BLK):
                load(j, j % Q)
            for q in range(Q):
                sp.wait_ge(y_scattered[q], 16 * len(range(q, BLK, Q)))
            for c in range(CH):
                sp.dma_start(yall[:, c], yrows[c * 2 * N:(c + 1) * 2 * N, :].rearrange("(t p k) h -> p t k h", p=P, k=2)
                             ).then_inc(y_loaded[c], 16)
            for c in range(CH):
                sp.wait_ge(second_added, c + 1)
                sp.dma_start(out.rearrange("b s d -> s b d")[:, c * TPC:(c + 1) * TPC, :],
                             x2[:, c * TPC:(c + 1) * TPC, :]).then_inc(out_stored, 16)
            sp.wait_ge(out_stored, 16 * CH)

        @block.scalar
        def _(act):
            act.dma_start(gam[:], ln_gamma.rearrange("(p o) -> p o", o=1)).then_inc(columns_loaded, 16)
            act.dma_start(bet[:], ln_beta.rearrange("(p o) -> p o", o=1)).then_inc(columns_loaded, 16)
            act.dma_start(b_rows[:], cond[0:L]).then_inc(columns_loaded, 16)
            act.wait_ge(memsets_done, 2)
            nc.scalar.activation(warm[:], mhalf[:, 0:1], ACT.Tanh)
            act.dma_start(fw_raw[:], fusion_w.rearrange("o (d i) -> o d i", d=2)).then_inc(fusion_loaded, 16)
            act.dma_start(fb_row[:], fusion_b.rearrange("(o p) -> o p", o=1)).then_inc(fusion_loaded, 16)
            act.dma_start(gw[:], gate_w).then_inc(gate_loaded, 16)

            def copy_x0T(c):
                act.wait_ge(x_transposed, c + 1)
                nc.scalar.copy(x0T[:, c * N:(c + 1) * N], pR[c % 2][:]).then_inc(x_normed_T_ready, 1)

            def tanhs(k):
                l, p = layer(k), pidx(k)
                act.wait_ge(u_ready, p + 1)
                if p >= NB:
                    act.wait_ge(drive_ready, p - NB + 1)
                    act.wait_ge(decay_raw, last_unit(p - NB) + 1)
                if p == 0:
                    act.wait_ge(prep_copied, 2)
                if k == upper[0]:
                    act.wait_ge(prep_copied, 4)
                q = p % NB
                nc.scalar.activation(T1[:, q], pU[p % 2][:], ACT.Tanh, bias=b_full[:, l:l + 1]).then_inc(tanhs_done, 1)
                nc.scalar.activation(T2[:, q], pU[p % 2][:], ACT.Tanh, bias=b_half[:, l:l + 1], scale=-0.5
                                     ).then_inc(tanhs_done, 1)

            def centre(k):
                l = layer(k)
                act.wait_ge(centred, k + 1)
                after(act, n_ready, k - NB + 1)
                after(act, variance_ready, k - NB + 1)
                q = k % NB
                nc.scalar.activation(SQ[:, q], pC[k % 2][:], ACT.Square, bias=cb[:, l:l + 1]).then_inc(squared, 1)
                nc.scalar.activation(CS[:, q], pC[k % 2][:], ACT.Identity, bias=cb[:, l:l + 1]).then_inc(cent_ready, 1)

            def split_high(i):
                act.wait_ge(experts_loaded[i % 2], 16 * (i // 2 + 1))
                nc.scalar.activation(split_part(i, 0), staged(i), ACT.Copy).then_inc(high_ready, 1)

            def post_x2(c):
                act.wait_ge(fused, c + 1)
                nc.scalar.copy(x2[:, c * TPC:(c + 1) * TPC], post_bank[c][:].rearrange("p (t h) -> p t h", t=TPC)
                               ).then_inc(x2_ready, 1)

            def post_normed(c):
                tiles = slice(c * TPC, (c + 1) * TPC)
                act.wait_ge(scaled_mean_ready, c + 1)
                act.wait_ge(x2_ready, c + 1)
                for t in range(TPC):
                    ins = nc.scalar.activation(xr[:, 0, c * TPC + t, 0:H], x2[:, c * TPC + t], ACT.Identity,
                                               bias=nm[:, c, t:t + 1], scale=rs0[:, c * TPC + t:c * TPC + t + 1])
                ins.then_inc(x2_normed, 1)
                act.wait_ge(x2_normed, c + 1)
                nc.scalar.copy(xr[:, 1, tiles, 0:H], xr[:, 0, tiles, 0:H]).then_inc(second_rows_ready, 1)

            def post_transposed(c):
                act.wait_ge(x2_transposed, c + 1)
                nc.scalar.copy(x0T[:, c * N:(c + 1) * N], post_bank[c][:]).then_inc(x2_normed_T_ready, 1)

            def post_exp(c):
                act.wait_ge(gap_ready, c + 1)
                after(act, weights_ready, c)
                nc.scalar.activation(ratio[:], gap[:], ACT.Exp).then_inc(ratio_ready, 1)

            act.wait_ge(prep_products, 2)
            nc.scalar.copy(wt_raw[:], pX[:]).then_inc(wt_ready, 1)
            copy_x0T(0)
            act.wait_ge(memsets_done, 5)
            def posts(h):
                for c in chunks_at("turned", h):
                    post_transposed(c)
                for c in chunks_at("normed", h):
                    post_normed(c)
                for c in chunks_at("exp", h):
                    post_exp(c)
                for c in chunks_at("x2", h):
                    post_x2(c)

            for s in range(STEPS):
                if 1 <= s < CH:
                    copy_x0T(s)
                posts(2 * s)
                for k in projected_in(s):
                    tanhs(k)
                posts(2 * s + 1)
                if 0 <= s - 2 < K:
                    centre(s - 2)
                if 6 <= s < 6 + 2 * E:
                    split_high(s - 6)
            nc.scalar.activation(warm[:], mhalf[:, 0:1], ACT.Gelu)
            act.wait_ge(table_ready, 1)
            for e in range(1, E, 2):
                at = act.value_load(prow[0:1, e:e + 1], min_val=0, max_val=E * REG)
                act.dma_start(rows[bass.ds(at, P), :], pad[:, e, :]).then_inc(pads_stored, 16)

            def step(s, u):
                if has(s, 0):
                    act.wait_ge(xb_transposed, s + 1)
                    after(act, up_ready, s - 1)
                    nc.scalar.activation(xh[:, u % 2], banks[u % 2][:, 0:P], ACT.Copy).then_inc(xh_ready, 1)
                if has(s, 1):
                    act.wait_ge(up_ready, s)
                    after(act, g_transposed, s - 2)
                    nc.scalar.activation(g[:, (u - 1) % 2], banks[2 + (u - 1) % 2][:], ACT.Gelu).then_inc(g_ready, 1)
                if has(s, 2):
                    act.wait_ge(g_transposed, s - 1)
                    after(act, down_ready, s - 3)
                    nc.scalar.activation(gh[:, u % 2], banks[4 + u % 2][:], ACT.Copy).then_inc(gh_ready, 1)
                if has(s, 3):
                    q = (u - 3) % 2
                    act.wait_ge(down_ready, s - 2)
                    act.wait_ge(meta_ready, s - 2)
                    after(act, y_ready, s - 4)
                    nc.scalar.activation(yl[:, q], banks[6 + q][:, H:2 * H], ACT.Copy, scale=meta[:, (u - 3) % Q, 1:2]
                                         ).then_inc(y_low_ready, 1)

            block_steps(act, step)

        @block.gpsimd
        def _(pool):
            nc.gpsimd.memset(ident[:], 0.0).then_inc(memsets_done, 1)
            nc.gpsimd.memset(mhalf[:], -0.5).then_inc(memsets_done, 1)
            nc.gpsimd.memset(inv_h[:], 1.0 / H).then_inc(memsets_done, 1)
            nc.gpsimd.memset(ones_row[:], 1.0).then_inc(memsets_done, 1)
            nc.gpsimd.memset(cb[:], 0.0).then_inc(memsets_done, 1)
            pool.wait_ge(memsets_done, 5)
            nc.gpsimd.affine_select(out=ident[:], in_=ident[:], compare_op=ALU.not_equal, fill=1.0, base=0,
                                    pattern=[[-1, P]], channel_multiplier=1).then_inc(constants_ready, 1)

            nc.gpsimd.memset(ones_bf[:], 1.0).then_inc(memsets_done, 1)
            nc.gpsimd.memset(ones8[:], 1.0).then_inc(memsets_done, 1)
            nc.gpsimd.memset(pad[:], 0.0).then_inc(memsets_done, 1)
            pool.wait_ge(memsets_done, 8)
            nc.gpsimd.affine_select(out=before[:], in_=ones_bf[:], compare_op=ALU.is_gt, fill=0.0, base=0,
                                    pattern=[[1, P]], channel_multiplier=-1).then_inc(constants_ready, 1)
            loose = dict(allow_small_or_imprecise_dtypes=True)
            nc.gpsimd.iota(rank[:], pattern=[[0, 2], [0, TPC], [-1, E]], base=E, channel_multiplier=0, **loose
                           ).then_inc(constants_ready, 1)
            nc.gpsimd.iota(eoff[:], pattern=[[0, TPC], [REG, E]], base=0, channel_multiplier=0, **loose
                           ).then_inc(constants_ready, 1)
            nc.gpsimd.iota(c128[:], pattern=[[0, E], [P, B]], base=0, channel_multiplier=0, **loose
                           ).then_inc(constants_ready, 1)

            def power0(c, count, counted):
                pool.wait_ge(counted, count)
                nc.gpsimd.tensor_tensor(rs0[:, c * TPC:(c + 1) * TPC], vpe[:, c * TPC:(c + 1) * TPC],
                                        mhalf[:], ALU.pow).then_inc(token_rstd, 1)

            for c in range(CH - 1):
                power0(c, c + 1, x_stats)

            def routing_constants():
                nc.gpsimd.iota(jj[:], pattern=[[1, BLK], [0, E]], base=0, channel_multiplier=0, **loose
                               ).then_inc(constants_ready, 1)
                for k in range(2):
                    nc.gpsimd.iota(xr[:, k, :, DEST].bitcast(U32), pattern=[[2 * P, B]], base=k, channel_multiplier=2
                                   ).then_inc(constants_ready, 1)
                nc.gpsimd.iota(pad[:, :, DEST].bitcast(U32), pattern=[[P, E + DUMMY]], base=2 * B * P, channel_multiplier=1
                               ).then_inc(pads_written, 1)

            def decay(k):
                p = pidx(k)
                pool.wait_ge(tanhs_done, 2 * p + 2)
                after(pool, resid_ready, k - NB + 1)
                nc.gpsimd.tensor_scalar(Ab[:, k % NB], T2[:, p % NB], 0.5, 0.5, ALU.mult, ALU.add
                                        ).then_inc(decay_raw, 1)

            def power(k):
                pool.wait_ge(var_eps_ready, k + 1)
                after(pool, rstd_spread, k - NB + 1)
                nc.gpsimd.tensor_tensor(rs[:, k % NB], ve[:, k % NB], mhalf[:], ALU.pow).then_inc(rstd_ready, 1)

            def split(i):
                pool.wait_ge(high_ready, i + 1)
                nc.gpsimd.tensor_tensor(split_part(i, 1), staged(i), split_part(i, 0).bitcast(F32), ALU.subtract
                                        ).then_inc(split_ready, 1)

            def scatter(c, first, count):
                pool.wait_ge(slots_ready, c + 1)
                pool.wait_ge(weights_ready, c + 1)
                pool.wait_ge(second_rows_ready, c + 1)
                for i in range(first, first + count):
                    k, t = i // TPC, i % TPC
                    nc.gpsimd.indirect_dma_start(rows[:], bass.IndirectOffsetOnAxis(slot[:, c, k, t:t + 1], 0),
                                                 xr[:, k, c * TPC + t, :], None).then_inc(rows_scattered, 16)

            def posts(h):
                for c in chunks_at("rstd", h):
                    power0(c, c + 1, x2_stats)
                    pool.wait_ge(neg_mean_ready, c + 1)
                    pool.wait_ge(token_rstd, CH + c + 1)
                    nc.gpsimd.tensor_tensor(nm[:, c], negmu[:, c], rs0[:, c * TPC:(c + 1) * TPC], ALU.mult
                                            ).then_inc(scaled_mean_ready, 1)
                for i in range(2 * TPC):
                    if 0 in chunks_at("scatter", h - 2 * i):
                        scatter(0, i, 1)
                for i in range(2):
                    for c in chunks_at("scatter", h - i):
                        if c > 0:
                            scatter(c, i * TPC, TPC)

            for s in range(STEPS):
                posts(2 * s)
                if s < K:
                    decay(s)
                if s == 0:
                    power0(CH - 1, CH, x_stats)
                if s == 5:
                    routing_constants()
                posts(2 * s + 1)
                if 0 <= s - 3 < K:
                    power(s - 3)
                if 6 <= s < 6 + 2 * E:
                    split(s - 6)

            for j in range(BLK):
                q = j % Q
                pool.wait_ge(y_ready, j + 1)
                nc.gpsimd.indirect_dma_start(yrows[:], bass.IndirectOffsetOnAxis(meta[:, q, 0:1].bitcast(U32), 0),
                                             yb[:, q, :], None).then_inc(y_scattered[q], 16)

        @block.vector
        def _(dve):
            steps = [0]

            def done(ins):
                steps[0] += 1
                ins.then_inc(vector_steps, 1)

            def link(ins):
                done(ins)
                dve.wait_ge(vector_steps, steps[0])

            def layernorm(src, c):
                for t in range(c * TPC, (c + 1) * TPC):
                    done(nc.vector.bn_stats(stats[:, t], src[:, t]))
                dve.wait_ge(vector_steps, steps[0])
                for t in range(c * TPC, (c + 1) * TPC):
                    done(nc.vector.bn_aggr(mv[:, t], stats[:, t]))
                dve.wait_ge(vector_steps, steps[0])
                return nc.vector.tensor_scalar(vpe[:, c * TPC:(c + 1) * TPC], mv[:, c * TPC:(c + 1) * TPC, 1], LN_EPS,
                                               None, ALU.add)

            def normed(dst, src, c, count):
                dve.wait_ge(token_rstd, count)
                for t in range(c * TPC, (c + 1) * TPC):
                    ins = nc.vector.tensor_scalar(dst(t), src[:, t], mv[:, t, 0:1], rs0[:, t:t + 1],
                                                  ALU.subtract, ALU.mult)
                return ins

            def drive(k):
                p = pidx(k)
                dve.wait_ge(tanhs_done, 2 * p + 2)
                q = p % NB
                nc.vector.scalar_tensor_tensor(out=Bb[:, q], in0=T2[:, q], scalar=-1.0, in1=T1[:, q],
                                               op0=ALU.add, op1=ALU.mult).then_inc(drive_ready, 1)

            def clip(k):
                q = k % NB
                dve.wait_ge(decay_raw, k + 1)
                nc.vector.tensor_scalar(Ab[:, q], Ab[:, q], CLAMP_LO, CLAMP_HI, ALU.max, ALU.min
                                        ).then_inc(decay_clipped, 1)

            def reset(k):
                dve.wait_ge(decay_clipped, k + 1)
                q = k % NB
                first = 0 if k % 2 == 0 else P - 1
                nc.vector.memset(Ab[:, q, first::P], 0.0).then_inc(decay_ready, 1)

            def scan(k):
                p = pidx(k)
                dve.wait_ge(drive_ready, p + 1)
                dve.wait_ge(decay_ready, k + 1)
                after(dve, centred, k - NB + 1)
                q = k % NB
                way = slice(None) if k % 2 == 0 else slice(None, None, -1)
                a_, b_, o_ = (v[:, way] for v in (Ab[:, q], Bb[:, p % NB], R[:, q]))
                ins = nc.vector.tensor_tensor_scan(out=o_, data0=a_, data1=b_, initial=0.0, op0=ALU.mult, op1=ALU.add)
                if layer(k) == 0:
                    ins.then_inc(resid_ready, 1)
                else:
                    ins.then_inc(scanned, 1)

            def residual(k):
                q, d, c = k % NB, k % 2, chunk(k)
                dve.wait_ge(scanned, upper.index(k) + 1)
                nc.vector.scalar_tensor_tensor(out=R[:, q], in0=n[:, d, c * N:(c + 1) * N], scalar=gam2[:],
                                               in1=R[:, q], op0=ALU.mult, op1=ALU.add).then_inc(resid_ready, 1)

            def addeps(k):
                dve.wait_ge(variance_ready, k + 1)
                after(dve, rstd_ready, k - NB + 1)
                nc.vector.tensor_scalar(ve[:, k % NB], pV[:, 0:TPC], 4 * LN_EPS, None, ALU.add
                                        ).then_inc(var_eps_ready, 1)

            def norm(k):
                q, d, c = k % NB, k % 2, chunk(k)
                dve.wait_ge(rstd_spread, k + 1)
                dve.wait_ge(cent_ready, k + 1)
                nc.vector.tensor_tensor(n[:, d, c * N:(c + 1) * N], CS[:, q], pR[k % 2][:], ALU.mult
                                        ).then_inc(n_ready, 1)

            def post_stats(c):
                dve.wait_ge(x2_ready, c + 1)
                layernorm(x2, c).then_inc(x2_stats, 1)
                nc.vector.tensor_scalar(negmu[:, c], mv[:, c * TPC:(c + 1) * TPC, 0], -1.0, None, ALU.mult
                                        ).then_inc(neg_mean_ready, 1)

            def post_route(c):
                tiles = slice(c * TPC, (c + 1) * TPC)
                dve.wait_ge(logits_ready, c + 1)
                lg = post_bank[c][:, 0:TPC * E].rearrange("p (t e) -> p t e", e=E)
                for t in range(TPC):
                    done(nc.vector.max(top8[:, t], lg[:, t]))
                dve.wait_ge(vector_steps, steps[0])
                nc.vector.tensor_tensor(gap[:], top8[:, :, 1], top8[:, :, 0], ALU.subtract).then_inc(gap_ready, 1)
                for k in range(2):
                    ins = nc.vector.tensor_tensor(tied[:, k], lg, top8[:, :, k:k + 1].to_broadcast([P, TPC, E]), ALU.is_equal)
                    done(ins)
                dve.wait_ge(vector_steps, steps[0])
                link(nc.vector.tensor_tensor(tied[:], tied[:], rank[:], ALU.mult))
                for k in range(2):
                    if k == 1:
                        link(nc.vector.scalar_tensor_tensor(out=tied[:, 1], in0=oh[:, 0], scalar=0.0, in1=tied[:, 1],
                                                            op0=ALU.is_equal, op1=ALU.mult))
                    link(nc.vector.tensor_reduce(best[:, k], tied[:, k], AX_X, ALU.max))
                    link(nc.vector.tensor_tensor(oh[:, k], tied[:, k], best[:, k].unsqueeze(2).to_broadcast([P, TPC, E]),
                                                 ALU.is_equal))
                nc.vector.tensor_tensor(M[:, tiles], oh[:, 0], oh[:, 1], ALU.add).then_inc(chosen_ready, 1)
                dve.wait_ge(chosen_ready, c + 1)
                with nc.allow_low_precision(reason="sums of four ones"):
                    nc.vector.tensor_reduce(Msum[:, c], M[:, tiles].rearrange("p t e -> p e t"), AX_X, ALU.add
                                            ).then_inc(chunk_counted, 1)

            def post_slots(c):
                dve.wait_ge(positions_ready, c + 1)
                pos = post_bank[c][:, 0:TPC * E].rearrange("p (t e) -> p t e", e=E)
                link(nc.vector.tensor_tensor(place[:], pos, eoff[:], ALU.add))
                link(nc.vector.tensor_tensor(picked[:], oh[:], place[:].unsqueeze(1).to_broadcast([P, 2, TPC, E]), ALU.mult))
                with nc.allow_low_precision(reason="whole numbers, one of them other than zero"):
                    nc.vector.tensor_reduce(slot[:, c], picked[:], AX_X, ALU.add).then_inc(slots_ready, 1)

            def post_weights(c):
                tiles = slice(c * TPC, (c + 1) * TPC)
                dve.wait_ge(ratio_ready, c + 1)
                link(nc.vector.tensor_scalar(total[:], ratio[:], 1.0, None, ALU.add))
                link(nc.vector.reciprocal(xr[:, 0, tiles, WGT], total[:]))
                nc.vector.tensor_tensor(xr[:, 1, tiles, WGT], ratio[:], xr[:, 0, tiles, WGT], ALU.mult
                                        ).then_inc(weights_ready, 1)

            def stats0(c):
                dve.wait_ge(x_loaded[c], 16)
                layernorm(xt, c).then_inc(x_stats, 1)

            def normed0(c):
                normed(lambda t: x0[:, t], xt, c, c + 1).then_inc(x_normed, 1)

            stats0(0)
            dve.wait_ge(columns_loaded, 48)
            dve.wait_ge(constants_ready, 1)
            done(nc.vector.tensor_scalar(ngam[:], gam[:], -1.0, None, ALU.mult))
            done(nc.vector.tensor_scalar(gam2[:], gam[:], 2.0, None, ALU.mult))
            nc.vector.tensor_scalar(cmat[:], ident[:], -1.0 / H, None, ALU.add).then_inc(prep_copied, 1)
            normed0(0)
            dve.wait_ge(prep_products, 1)
            link(nc.vector.tensor_copy(b_full[:, 0:1], pV[:, 0:1]))
            done(nc.vector.tensor_copy(b_raw[:], pV[:, 0:L]))
            nc.vector.tensor_scalar(b_half[:, 0:1], b_full[:, 0:1], -0.5, None, ALU.mult).then_inc(prep_copied, 1)
            stats0(1)
            stats0(2)
            normed0(1)
            stats0(3)
            normed0(2)

            def posts(h):
                for c in chunks_at("slots", h):
                    post_slots(c)
                    post_weights(c)
                for c in chunks_at("route", h):
                    post_route(c)
                for c in chunks_at("stats", h):
                    post_stats(c)

            for s in range(STEPS):
                posts(2 * s)
                if 0 <= s - 1 < K:
                    clip(s - 1)
                    if s - 1 in projected:
                        drive(s - 1)
                    reset(s - 1)
                    scan(s - 1)
                posts(2 * s + 1)
                if 0 <= s - 3 < K:
                    addeps(s - 3)
                if s - 1 in upper:
                    residual(s - 1)
                if 0 <= s - 4 < K:
                    norm(s - 4)
                if s == 3:
                    dve.wait_ge(wt_ready, 1)
                    link(nc.vector.tensor_scalar(wt_g[:], wt_raw[:], ngam[:], None, ALU.mult))
                if s == 1:
                    normed0(3)
                if s == 2:
                    dve.wait_ge(prep_products, 3)
                    link(nc.vector.tensor_copy(fwt_raw[:], pX[:, 0:2 * H].rearrange("p (d o) -> p d o", d=2)))
                    nc.vector.tensor_scalar(fwt_g[:], fwt_raw[:], ngam[:], None, ALU.mult).then_inc(prep_copied, 1)
                if s == 4:
                    dve.wait_ge(prep_products, 4)
                    done(nc.vector.tensor_scalar(cb[:, 1:L], pX[:, L:L + 1].to_broadcast([P, L - 1]), -2.0, None, ALU.mult))
                    link(nc.vector.tensor_tensor(b_full[:, 1:L], pX[:, 1:L], b_raw[:, 1:L], ALU.add))
                    nc.vector.tensor_scalar(b_half[:, 1:L], b_full[:, 1:L], -0.5, None, ALU.mult
                                            ).then_inc(prep_copied, 1)
                if s == 6:
                    dve.wait_ge(prep_products, 5)
                    link(nc.vector.tensor_copy(fbias[:], pX[:, 0:H]))
                if 7 <= s < 7 + CH:
                    tiles = slice((s - 7) * TPC, (s - 6) * TPC)
                    nc.vector.tensor_tensor(xt[:, tiles], xt[:, tiles],
                                            fbias[:].unsqueeze(1).to_broadcast([P, TPC, H]), ALU.add
                                                               ).then_inc(x_biased, 1)
                if s == unit(L - 1, 0, 1) + 1:
                    dve.wait_ge(constants_ready, 8)

            dve.wait_ge(experts_counted, 1)
            link(nc.vector.tensor_copy(cnt[:], post_bank[0][0:1, 0:E]))
            nc.vector.tensor_tensor(prow[:], cnt[:], eoff[0:1, 0], ALU.add).then_inc(table_ready, 1)
            link(nc.vector.tensor_tensor(gtc[:], cnt[:].unsqueeze(2).to_broadcast([1, E, B]), c128[:], ALU.is_gt))
            link(nc.vector.tensor_reduce(nblk[:], gtc[:], AX_X, ALU.add))
            done(nc.vector.tensor_scalar(dlt[:], nblk[:], -float(P), float(REG), ALU.mult, ALU.add))
            link(nc.vector.tensor_tensor_scan(out=endb[:], data0=ones8[:], data1=nblk[:], initial=0.0,
                                              op0=ALU.mult, op1=ALU.add))
            link(nc.vector.tensor_tensor(ge[:], jj[:], endb[:].unsqueeze(1).to_broadcast([1, BLK, E]), ALU.is_ge))
            link(nc.vector.tensor_reduce(tj[:], ge[:], AX_X, ALU.add))
            done(nc.vector.tensor_scalar(eid[:], tj[:], float(E - 1), None, ALU.min))
            link(nc.vector.tensor_tensor(ge[:], ge[:], dlt[:].unsqueeze(1).to_broadcast([1, BLK, E]), ALU.mult))
            link(nc.vector.tensor_reduce(tr_[:], ge[:], AX_X, ALU.add))
            nc.vector.scalar_tensor_tensor(out=brow[:], in0=jj[:, :, 0], scalar=float(P), in1=tr_[:],
                                           op0=ALU.mult, op1=ALU.add).then_inc(table_ready, 1)

            def step(s, u):
                if has(s, 0):
                    dve.wait_ge(xh_ready, s + 1)
                    nc.vector.tensor_tensor(xl[:, u % 2], banks[u % 2][:, 0:P], xh[:, u % 2].bitcast(F32),
                                            ALU.subtract).then_inc(xl_ready, 1)
                    after(dve, y_scattered[u], (16 // Q) * (s - u))
                    nc.vector.tensor_copy(meta[:, u], xb[:, u, H:RW]).then_inc(meta_ready, 1)
                if has(s, 2):
                    dve.wait_ge(gh_ready, s - 1)
                    nc.vector.tensor_tensor(gl[:, u % 2], banks[4 + u % 2][:], gh[:, u % 2].bitcast(F32),
                                            ALU.subtract).then_inc(gl_ready, 1)
                if has(s, 3):
                    q = (u - 3) % Q
                    dve.wait_ge(y_low_ready, s - 2)
                    nc.vector.scalar_tensor_tensor(out=yb[:, q], in0=banks[6 + (u - 3) % 2][:, 0:H],
                                                   scalar=meta[:, q, 1:2], in1=yl[:, (u - 3) % 2],
                                                   op0=ALU.mult, op1=ALU.add).then_inc(y_ready, 1)

            block_steps(dve, step)
            for c in range(CH):
                tiles = slice(c * TPC, (c + 1) * TPC)
                dve.wait_ge(y_loaded[c], 16)
                nc.vector.tensor_tensor(x2[:, tiles], x2[:, tiles], yall[:, c, :, 0], ALU.add).then_inc(first_added, 1)
                dve.wait_ge(first_added, c + 1)
                nc.vector.tensor_tensor(x2[:, tiles], x2[:, tiles], yall[:, c, :, 1], ALU.add).then_inc(second_added, 1)

        @block.tensor
        def _(pe):
            mm, tr = nc.tensor.matmul, nc.tensor.transpose

            def transpose_x0(c):
                pe.wait_ge(x_normed, c + 1)
                after(pe, x_normed_T_ready, c - 1)
                for t in range(TPC):
                    ins = tr(pR[c % 2][:, t * P:(t + 1) * P], x0[:, c * TPC + t, :], ident[:])
                ins.then_inc(x_transposed, 1)

            pe.wait_ge(constants_ready, 1)
            pe.wait_ge(columns_loaded, 48)
            mm(pV[:, 0:L], b_rows[:], ident[0:L, 0:L], start=True, stop=True).then_inc(prep_products, 1)
            pe.wait_ge(w_loaded, 16)
            for l in range(L):
                ins = tr(pX[:, l * H:(l + 1) * H], w_raw[:, l, :], ident[:])
            ins.then_inc(prep_products, 1)
            transpose_x0(0)

            def project(k):
                l, p, d, c = layer(k), pidx(k), k % 2, chunk(k)
                if l == 0:
                    pe.wait_ge(x_normed_T_ready, c + 1)
                    src, wt = x0T[:, c * N:(c + 1) * N], wt_raw
                else:
                    pe.wait_ge(n_ready, below(k) + 1)
                    src, wt = n[:, d, c * N:(c + 1) * N], wt_g
                after(pe, tanhs_done, 2 * (p - 1))
                if k == 0:
                    pe.wait_ge(wt_ready, 1)
                mm(pU[p % 2][:], wt[:, l * H:(l + 1) * H], src, start=True, stop=True).then_inc(u_ready, 1)

            def centre(k):
                if k == 0:
                    pe.wait_ge(prep_copied, 1)
                pe.wait_ge(resid_ready, k + 1)
                after(pe, cent_ready, k - 1)
                mm(pC[k % 2][:], cmat[:], R[:, k % NB], start=True, stop=True).then_inc(centred, 1)

            def variance(k):
                pe.wait_ge(squared, k + 1)
                after(pe, var_eps_ready, k)
                for t in range(TPC):
                    ins = mm(pV[:, t:t + 1], SQ[:, k % NB, t * P:(t + 1) * P], inv_h[:], start=True, stop=True)
                ins.then_inc(variance_ready, 1)

            def spread(k):
                pe.wait_ge(rstd_ready, k + 1)
                after(pe, n_ready, k - 1)
                if k == 0:
                    pe.wait_ge(x_normed_T_ready, CH)
                for t in range(TPC):
                    ins = mm(pR[k % 2][:, t * P:(t + 1) * P], rs[:, k % NB, t:t + 1].to_broadcast([P, P]), ident[:],
                             start=True, stop=True)
                ins.then_inc(rstd_spread, 1)

            def fuse(c):
                pe.wait_ge(n_ready, unit(L - 1, c, 1) + 1)
                if c == 0:
                    pe.wait_ge(x_biased, CH)
                if c % 2:
                    pe.wait_ge(tanhs_done, 2 * len(projected))
                if c == 2:
                    pe.wait_ge(slots_ready, 1)
                mm(post_bank[c][:], ident[:], xt[:, c * TPC:(c + 1) * TPC].rearrange("p t h -> p (t h)"),
                   start=True, stop=False)
                for t in range(TPC):
                    for d in range(2):
                        ins = mm(post_bank[c][:, t * H:(t + 1) * H], n[:, d, (c * TPC + t) * P:(c * TPC + t + 1) * P],
                                 fwt_g[:, d, :], start=False, stop=(t == TPC - 1 and d == 1))
                ins.then_inc(fused, 1)

            def post_transpose(c):
                pe.wait_ge(x2_normed, c + 1)
                for t in range(TPC):
                    ins = tr(post_bank[c][:, t * P:(t + 1) * P], xr[:, 0, c * TPC + t, 0:H], ident[:])
                ins.then_inc(x2_transposed, 1)

            def post_logits(c):
                pe.wait_ge(gate_loaded, 16)
                pe.wait_ge(x2_normed_T_ready, c + 1)
                for t in range(TPC):
                    ins = mm(post_bank[c][:, t * E:(t + 1) * E], x0T[:, (c * TPC + t) * P:(c * TPC + t + 1) * P], gw[:],
                             start=True, stop=True)
                ins.then_inc(logits_ready, 1)

            def post_positions(c):
                pe.wait_ge(constants_ready, 2)
                pe.wait_ge(chosen_ready, c + 1)
                tiles = slice(c * TPC, (c + 1) * TPC)
                mm(post_bank[c][:, 0:TPC * E], before[:], M[:, tiles].rearrange("p t e -> p (t e)"), start=True, stop=False)
                for t in range(TPC - 1):
                    ins = mm(post_bank[c][:, (t + 1) * E:TPC * E], ones_bf[:],
                             M[:, c * TPC + t:c * TPC + t + 1].to_broadcast([P, TPC - 1 - t, E]),
                             start=False, stop=(c == 0 and t == TPC - 2))
                after(pe, chunk_counted, c)
                for b in range(c):
                    ins = mm(post_bank[c][:, 0:TPC * E], ones_bf[:], Msum[:, b:b + 1].to_broadcast([P, TPC, E]),
                             start=False, stop=(b == c - 1))
                ins.then_inc(positions_ready, 1)

            def posts(h):
                for c in chunks_at("positions", h):
                    post_positions(c)
                for c in chunks_at("logits", h):
                    post_logits(c)
                for c in chunks_at("turn", h):
                    post_transpose(c)
                for c in chunks_at("fuse", h):
                    fuse(c)

            for s in range(STEPS):
                posts(2 * s)
                for k in projected_in(s):
                    project(k)
                if 0 <= s - 2 < K:
                    centre(s - 2)
                posts(2 * s + 1)
                if 0 <= s - 3 < K:
                    variance(s - 3)
                if 0 <= s - 4 < K:
                    spread(s - 4)
                if 0 <= s < CH - 1:
                    transpose_x0(s + 1)
                if s == 1:
                    pe.wait_ge(fusion_loaded, 32)
                    for d in range(2):
                        ins = tr(pX[:, d * H:(d + 1) * H], fw_raw[:, d, :], ident[:])
                    ins.then_inc(prep_products, 1)
                if s == 3:
                    pe.wait_ge(prep_copied, 3)
                    for l in range(1, L):
                        mm(pX[:, l:l + 1], wt_raw[:, l * H:(l + 1) * H], bet[:], start=True, stop=True)
                    mm(pX[:, L:L + 1], cmat[:], bet[:], start=True, stop=True).then_inc(prep_products, 1)
                if s == 6:
                    pe.wait_ge(prep_copied, 4)
                    for d in range(2):
                        mm(pX[:, 0:H], bet[:].to_broadcast([P, P]), fwt_raw[:, d, :], start=(d == 0), stop=False)
                    mm(pX[:, 0:H], ones_row[:], fb_row[:], start=False, stop=True).then_inc(prep_products, 1)
            pe.wait_ge(slots_ready, 3)
            for c in range(CH):
                pe.wait_ge(chunk_counted, c + 1)
                ins = mm(post_bank[0][:, 0:E], ones_bf[:], Msum[:, c], start=(c == 0), stop=(c == CH - 1))
            ins.then_inc(experts_counted, 1)

            pe.wait_ge(split_ready, 2 * E)
            pe.wait_ge(table_ready, 2)
            pe.wait_ge(slots_ready, 4)

            experts = {}

            def expert(s, u, d):
                if d == 1 or u < 2:
                    experts[(u - d) % Q] = pe.value_load(eid[0:1, bass.ds(s - d, 1)], min_val=0, max_val=E - 1)
                return experts[(u - d) % Q]

            def step(s, u):
                if has(s, 1):
                    e = expert(s, u, 1)
                if has(s, 0):
                    q = u % Q
                    pe.wait_ge(xb_loaded[q], (16 // Q) * (s - q) + 16)
                    tr(banks[q % 2][:, 0:P], xb[:, q, 0:H], ident[:]).then_inc(xb_transposed, 1)
                if has(s, 1):
                    q = (u - 1) % 2
                    pe.wait_ge(xl_ready, s)
                    mm(banks[2 + q][:], xh[:, q], w1s[:, :, 0][:, bass.ds(e, 1)], start=True, stop=False)
                    mm(banks[2 + q][:], xh[:, q], w1s[:, :, 1][:, bass.ds(e, 1)], start=False, stop=False)
                    mm(banks[2 + q][:], xl[:, q], w1s[:, :, 0][:, bass.ds(e, 1)], start=False, stop=True
                       ).then_inc(up_ready, 1)
                if has(s, 3):
                    e = expert(s, u, 3)
                if has(s, 2):
                    q = (u - 2) % 2
                    pe.wait_ge(g_ready, s - 1)
                    for f in range(FC):
                        ins = tr(banks[4 + q][:, f * P:(f + 1) * P], g[:, q, f * P:(f + 1) * P], ident[:])
                    ins.then_inc(g_transposed, 1)
                if has(s, 3):
                    q = (u - 3) % 2
                    pe.wait_ge(gl_ready, s - 2)
                    after(pe, y_ready, s - 4)
                    for f in range(FC):
                        cols = slice(f * P, (f + 1) * P)
                        both = w2s[:, :, f].rearrange("p e k c -> p e (k c)")
                        mm(banks[6 + q][:, 0:2 * H], gh[:, q, cols], both[:, bass.ds(e, 1)], start=(f == 0), stop=False)
                        ins = mm(banks[6 + q][:, 0:H], gl[:, q, cols], both[:, :, 0:H][:, bass.ds(e, 1)],
                                 start=False, stop=(f == FC - 1))
                    ins.then_inc(down_ready, 1)

            block_steps(pe, step)


_INS = ["x", "ctx_1024", "cond_1024", "L0_xcond_fusion_W", "L0_xcond_fusion_b", "L0_xcond_ln_gamma", "L0_xcond_ln_beta",
        "L0_ffn_gate_w", "L0_ffn_w1", "L0_ffn_w2"]


def kernel(**inputs):
    import numpy as np
    import concourse.bacc as bacc
    from concourse.bass_utils import run_bass_kernel_spmd

    nc = bacc.Bacc("TRN2", target_bir_lowering=False, num_devices=1)
    arrays, args = {}, []
    for name in _INS:
        a = np.ascontiguousarray(inputs[name])
        arrays[f"in_{name}"] = a
        args.append(nc.dram_tensor(f"in_{name}", a.shape, mybir.dt.from_np(a.dtype), kind="ExternalInput").ap())
    args.append(nc.dram_tensor("out", (B, P, H), F32, kind="ExternalOutput").ap())
    args.append(nc.dram_tensor("rows", (E * REG + DUMMY * P, RW), F32).ap())
    args.append(nc.dram_tensor("yrows", ((2 * B + E + DUMMY) * P, H), F32).ap())
    program(nc, *args)
    return run_bass_kernel_spmd(nc, [arrays], core_ids=[0]).results[0]["out"]
```
